# Optimizing a Trainium2 kernel written in Bass

```python
import numpy as np
import jax
import jax.numpy as jnp

def _softmax(x, axis=-1):
    return jax.nn.softmax(x, axis=axis)

def _gelu(x):
    return jax.nn.gelu(x, approximate=True)

def _silu(x):
    return jax.nn.silu(x)

def _sigmoid(x):
    return jax.nn.sigmoid(x)

def _layernorm(x, axis=-1, eps=1e-05):
    m = jnp.mean(x, axis=axis, keepdims=True)
    v = jnp.var(x, axis=axis, keepdims=True)
    return (x - m) / jnp.sqrt(v + eps)

def _scatter_add(tgt, idx, src, axis=0):
    return tgt.at[idx].add(src)

def _segment_sum(src, seg, n):
    return jax.ops.segment_sum(src, seg, n)
kernel_name = 'mk_xattn_ffn_d2_seqx_r4_e4c340'

def setup_inputs(seed: int=0):
    np.random.seed(seed)
    _w = jnp.asarray

    def _rec_inputs():
        import jax
        import jax.numpy as jnp
        _rk = jax.random.key(seed)
        x = -0.000125 + 0.9999 * jax.random.normal(jax.random.fold_in(_rk, 1), (2, 512, 1024), jnp.float32)
        _lenS = 512 - jax.random.randint(jax.random.fold_in(_rk, 7), (2,), 0, max(1, 512 // 4) + 1, jnp.int32)
        _lenS2 = 1024 - jax.random.randint(jax.random.fold_in(_rk, 8), (2,), 0, max(1, 1024 // 4) + 1, jnp.int32)
        _ctx_4096P = jax.random.normal(jax.random.fold_in(_rk, 11), (2, 16, 1024), jnp.float32)
        _ctx_4096c = jax.random.dirichlet(jax.random.fold_in(_rk, 511), 0.3 * jnp.ones((16,), jnp.float32), (2, 1024))
        _ctx_4096t = jnp.einsum('bsk,bkd->bsd', _ctx_4096c, _ctx_4096P)
        _ctx_4096t = _ctx_4096t * jax.lax.rsqrt(jnp.mean(jnp.square(_ctx_4096t)) + 1e-12) * 0.953939
        ctx_4096 = -5.72187e-05 + 0.999849 * (_ctx_4096t + 0.3 * jax.random.normal(jax.random.fold_in(_rk, 611), (2, 1024, 1024), jnp.float32))
        return (x, ctx_4096)
    x, ctx_4096 = _rec_inputs()

    def _L0_xattn_setup():
        import jax, jax.numpy as jnp
        import numpy as np
        QMIN = 0.0
        QMAX = 255.0

        def fake_quant(x, scale, zp):
            s = scale.reshape(())
            z = zp.reshape(())
            q = jnp.clip(jnp.round(x / s + z), QMIN, QMAX)
            return (q - z) * s
        key = jax.random.key(seed)
        k1, k2 = jax.random.split(key)
        B, M, K, N = (4, 512, 1024, 1024)
        x1 = jax.random.normal(k1, (B, M, K), dtype=jnp.float32)
        x2 = jax.random.normal(k2, (B, K, N), dtype=jnp.float32)
        x1_scale = jnp.full((1,), 8.0 / 255.0, dtype=jnp.float32)
        x1_zp = jnp.full((1,), 128.0, dtype=jnp.float32)
        x2_scale = jnp.full((1,), 8.0 / 255.0, dtype=jnp.float32)
        x2_zp = jnp.full((1,), 128.0, dtype=jnp.float32)
        return {'x1': x1, 'x2': x2, 'x1_scale': x1_scale, 'x1_zp': x1_zp, 'x2_scale': x2_scale, 'x2_zp': x2_zp}
    _L0_xattn_all = _L0_xattn_setup()
    _L0_xattn_in = {k: v for k, v in _L0_xattn_all.items() if k in ('x1_scale', 'x1_zp', 'x2_scale', 'x2_zp')}
    del _L0_xattn_all

    def _L0_ffn_setup():
        import jax, jax.numpy as jnp
        import numpy as np
        B, S, D_IN, D_OUT = (2, 512, 1024, 1024)
        E, K, R = (8, 2, 16)
        SCALING = 32.0 / 16.0
        key = jax.random.key(seed)
        ks = jax.random.split(key, 6)
        x = jax.random.normal(ks[0], (B, S, D_IN), dtype=jnp.float32)
        gate_w = jax.random.normal(ks[1], (E, D_IN), dtype=jnp.float32) * 0.02
        base_w = jax.random.normal(ks[2], (D_OUT, D_IN), dtype=jnp.float32) * 0.02
        base_b = jax.random.normal(ks[3], (D_OUT,), dtype=jnp.float32) * 0.02
        lora_A = jax.random.normal(ks[4], (E, R, D_IN), dtype=jnp.float32) * 0.02
        lora_B = jax.random.normal(ks[5], (E, D_OUT, R), dtype=jnp.float32) * 0.02
        return {'x': x, 'gate_w': gate_w, 'base_w': base_w, 'base_b': base_b, 'lora_A': lora_A, 'lora_B': lora_B}
    _L0_ffn_all = _L0_ffn_setup()
    _L0_ffn_in = {k: v for k, v in _L0_ffn_all.items() if k in ('gate_w', 'base_w', 'base_b', 'lora_A', 'lora_B')}
    del _L0_ffn_all

    def _L1_xattn_setup():
        import jax, jax.numpy as jnp
        import numpy as np
        key = jax.random.key(seed)
        k1, k2 = jax.random.split(key)
        B, Lq, Lk, D = (16, 256, 512, 1024)
        query = jax.random.normal(k1, (B, Lq, D), dtype=jnp.float32)
        key_t = jax.random.normal(k2, (B, Lk, D), dtype=jnp.float32)
        return {'query': query, 'key': key_t}
    _L1_xattn_all = _L1_xattn_setup()
    _L1_xattn_in = {k: v for k, v in _L1_xattn_all.items() if k in ()}
    del _L1_xattn_all

    def _L1_ffn_setup():
        import jax, jax.numpy as jnp
        import numpy as np
        B_, S, D_IN, D_OUT = (4, 512, 1024, 1024)
        N, RANK, ALPHA = (8, 16, 32)
        SCALE = ALPHA / RANK
        key = jax.random.key(seed)
        kx, ka, kb, kw, kbias = jax.random.split(key, 5)
        x = jax.random.normal(kx, (B_, S, D_IN), dtype=jnp.float32)
        lora_A = jax.random.normal(ka, (N, RANK, D_IN), dtype=jnp.float32) * (1.0 / np.sqrt(D_IN))
        lora_B = jax.random.normal(kb, (N, D_OUT, RANK), dtype=jnp.float32) * (1.0 / np.sqrt(RANK))
        W = jax.random.normal(kw, (D_OUT, D_IN), dtype=jnp.float32) * (1.0 / np.sqrt(D_IN))
        bias = jax.random.normal(kbias, (D_OUT,), dtype=jnp.float32) * 0.01
        lora_weights = jnp.full((N,), 1.0 / N, dtype=jnp.float32)
        return {'x': x, 'lora_A': lora_A, 'lora_B': lora_B, 'W': W, 'bias': bias, 'lora_weights': lora_weights}
    _L1_ffn_all = _L1_ffn_setup()
    _L1_ffn_in = {k: v for k, v in _L1_ffn_all.items() if k in ('lora_A', 'lora_B', 'W', 'bias', 'lora_weights')}
    del _L1_ffn_all
    return {'x': x, 'ctx_4096': ctx_4096, 'L0_xattn_x1_scale': _L0_xattn_in['x1_scale'], 'L0_xattn_x1_zp': _L0_xattn_in['x1_zp'], 'L0_xattn_x2_scale': _L0_xattn_in['x2_scale'], 'L0_xattn_x2_zp': _L0_xattn_in['x2_zp'], 'L0_ffn_gate_w': _L0_ffn_in['gate_w'], 'L0_ffn_base_w': _L0_ffn_in['base_w'], 'L0_ffn_base_b': _L0_ffn_in['base_b'], 'L0_ffn_lora_A': _L0_ffn_in['lora_A'], 'L0_ffn_lora_B': _L0_ffn_in['lora_B'], 'L1_ffn_lora_A': _L1_ffn_in['lora_A'], 'L1_ffn_lora_B': _L1_ffn_in['lora_B'], 'L1_ffn_W': _L1_ffn_in['W'], 'L1_ffn_bias': _L1_ffn_in['bias'], 'L1_ffn_lora_weights': _L1_ffn_in['lora_weights']}

def reference(x, ctx_4096, L0_xattn_x1_scale, L0_xattn_x1_zp, L0_xattn_x2_scale, L0_xattn_x2_zp, L0_ffn_gate_w, L0_ffn_base_w, L0_ffn_base_b, L0_ffn_lora_A, L0_ffn_lora_B, L1_ffn_lora_A, L1_ffn_lora_B, L1_ffn_W, L1_ffn_bias, L1_ffn_lora_weights):
    import jax
    import jax.numpy as jnp

    def _L0_xattn_ref(x1, x2, x1_scale, x1_zp, x2_scale, x2_zp):
        import jax, jax.numpy as jnp
        import numpy as np
        QMIN = 0.0
        QMAX = 255.0

        def fake_quant(x, scale, zp):
            s = scale.reshape(())
            z = zp.reshape(())
            q = jnp.clip(jnp.round(x / s + z), QMIN, QMAX)
            return (q - z) * s
        q1 = fake_quant(x1, x1_scale, x1_zp)
        q2 = fake_quant(x2, x2_scale, x2_zp)
        return jnp.matmul(q1, q2)

    def _L0_ffn_ref(x, gate_w, base_w, base_b, lora_A, lora_B):
        import jax, jax.numpy as jnp
        import numpy as np
        B, S, D_IN, D_OUT = (2, 512, 1024, 1024)
        E, K, R = (8, 2, 16)
        SCALING = 32.0 / 16.0
        gate_logits = jnp.einsum('bsd,ed->bse', x, gate_w)
        weights, selected = jax.lax.top_k(gate_logits, K)
        weights = jax.nn.softmax(weights.astype(jnp.float32), axis=2).astype(x.dtype)
        result = jnp.einsum('bsd,od->bso', x, base_w) + base_b
        w_full = jnp.sum(jax.nn.one_hot(selected, E, dtype=x.dtype) * weights[..., None], axis=2)
        low = jnp.einsum('bsd,erd->ebsr', x, lora_A)
        lora_out = jnp.einsum('ebsr,eor,bse->bso', low, lora_B, w_full)
        result = result + SCALING * lora_out
        return result

    def _L1_xattn_ref(query, key):
        import jax, jax.numpy as jnp
        import numpy as np
        a = jnp.einsum('bqd,bkd->bqk', query, key)
        e = jax.nn.softmax(a, axis=-1)
        c = jnp.einsum('bqk,bkd->bqd', e, key)
        return c

    def _L1_ffn_ref(x, lora_A, lora_B, W, bias, lora_weights):
        import jax, jax.numpy as jnp
        import numpy as np
        B_, S, D_IN, D_OUT = (4, 512, 1024, 1024)
        N, RANK, ALPHA = (8, 16, 32)
        SCALE = ALPHA / RANK
        h = jnp.einsum('bsd,nrd->nbsr', x, lora_A)
        coef = (SCALE * lora_weights)[:, None, None]
        lora_out = jnp.einsum('nbsr,nor->bso', h, lora_B * coef)
        base = jnp.einsum('bsd,od->bso', x, W) + bias
        return base + lora_out
    x = x + _L0_xattn_ref(_layernorm(x, axis=-1), ctx_4096, L0_xattn_x1_scale, L0_xattn_x1_zp, L0_xattn_x2_scale, L0_xattn_x2_zp)
    x = x + _L0_ffn_ref(_layernorm(x, axis=-1), L0_ffn_gate_w, L0_ffn_base_w, L0_ffn_base_b, L0_ffn_lora_A, L0_ffn_lora_B)
    x = x + _L1_xattn_ref(_layernorm(x, axis=-1), ctx_4096)
    x = x + _L1_ffn_ref(_layernorm(x, axis=-1), L1_ffn_lora_A, L1_ffn_lora_B, L1_ffn_W, L1_ffn_bias, L1_ffn_lora_weights)
    return x

_drawn_inputs = setup_inputs


def setup_inputs(seed=0):
    import zlib

    import numpy as np

    out = dict(_drawn_inputs(seed))
    spreads = {'L1_ffn_lora_weights': (0.125, 0.6)}
    factors = {'L0_ffn_gate_w': 8.0,
     'L0_ffn_base_b': 64.0,
     'L0_ffn_lora_A': 8.0,
     'L0_ffn_lora_B': 8.0,
     'L1_ffn_bias': 64.0}
    for name, (base, spread) in spreads.items():
        noise = np.random.default_rng([zlib.crc32(name.encode()), seed]).standard_normal(out[name].shape)
        drawn = base * np.exp(spread * noise) if base else spread * noise
        out[name] = jnp.asarray(drawn.astype(out[name].dtype))
    for name, factor in factors.items():
        out[name] = (out[name] * factor).astype(out[name].dtype)
    return out
```

```python
from concourse import mybir
from contextlib import ExitStack

F32 = mybir.dt.float32
F32R = mybir.dt.float32r
BF16 = mybir.dt.bfloat16
U32 = mybir.dt.uint32
ALU = mybir.AluOpType
ACT = mybir.ActivationFunctionType
AX = mybir.AxisListType


def two_layer_kernel(nc, x, ctx, ctx_t, q_scalars, gate_t, w0_t, b0, a0_t, bb0_t, a1_t, bb1_t, w1_t, b1, lora_w, out):
    P = nc.NUM_PARTITIONS
    BATCHES, ROWS, D = x.shape
    KT = D // P
    TILES = ROWS // P
    HALF = D // 2
    KH = KT // 2
    EXPERTS, RANK = 8, 16
    ER = EXPERTS * RANK
    TOP = 2
    SCALING = 2.0
    EPS = 1e-5
    QMAX = 255.0
    MID = 128.0
    MAGIC = 12582912.0
    QMM, FFN0, QK, PV, FFN1 = STAGES = range(5)
    JOBS = len(STAGES) * TILES
    RAW = 3

    def job(b, s, t):
        return JOBS * b + TILES * s + t

    def stage_of(n):
        b, r = divmod(n, JOBS)
        return b, r // TILES, r % TILES

    def row_no(n):
        b, s, t = stage_of(n)
        return (JOBS - TILES) * b + TILES * (s - 1) + t

    def tile_no(n):
        b, _, t = stage_of(n)
        return TILES * b + t

    def lora_no(n):
        b, s, t = stage_of(n)
        return 2 * TILES * b + TILES * (s == FFN1) + t

    def norm_no(n):
        b, s, t = stage_of(n)
        return TILES * b + t if s == QMM else 3 * TILES * b + TILES * {FFN0: 0, QK: 1, FFN1: 2}[s] + t

    def add_no(n):
        b, s, t = stage_of(n)
        return 3 * TILES * b + TILES * {QMM: 0, FFN0: 1, FFN1: 2}[s] + t

    N = JOBS * BATCHES
    has_lora = lambda s: s in (FFN0, FFN1)

    PER_WINDOW = {QMM: (("lora0a",), ("lora0b",), (), ()),
                  FFN0: (3, 3, 2, 0), QK: (3, 3, 2, 0), PV: (3, 3, 2, 0), FFN1: (4, 4, 4, 4)}
    MATRIX = {FFN0: ["kt"] * KT, QK: ["v"] * KT, PV: ["w1"] * KT, FFN1: ["q2"] * KT + ["w0"] * KT}
    units = []
    for b in range(BATCHES):
        for s in STAGES:
            todo = [(m, i % KT) for i, m in enumerate(MATRIX.get(s, []))]
            if s == FFN1 and b == BATCHES - 1:
                todo = []
            for t in range(TILES):
                n = job(b, s, t)
                if s == QMM:
                    units += [(n, m, b, 0) for m in PER_WINDOW[s][t]]
                    continue
                take, todo = todo[:PER_WINDOW[s][t]], todo[PER_WINDOW[s][t]:]
                units += [(n, m, b + (s == FFN1), k) for m, k in take]
                if s == QK and t == TILES - 1:
                    units += [(n, "lora1a", b, 0), (n, "lora1b", b, 0)]
    unit_no = {(m, b, k): u for u, (_, m, b, k) in enumerate(units)}
    window_units = {n: [u for u, w in enumerate(units) if w[0] == n] for n in range(-1, N)}

    es = ExitStack()
    with es:
        at = [(nc.sbuf_base + 31) // 32 * 32]
        size = {F32: 4, F32R: 4, BF16: 2, U32: 4}

        def place(name, shape, dt, over=None):
            if over is None:
                over = at[0]
                n = size[dt]
                for d in shape[1:]:
                    n *= d
                at[0] += (n + 31) // 32 * 32
            return nc.alloc_sbuf_tensor_at(name, shape, dt, offset=over), over

        x_sb, _ = place("x_sb", [P, TILES, D], F32)
        r0_hi, _ = place("r0_hi", [P, KT, D], F32R)
        r0_lo, _ = place("r0_lo", [P, KT, D], F32R)
        r1_hi, r1_hi_at = place("r1_hi", [P, KT, D], F32R)
        r1_lo, r1_lo_at = place("r1_lo", [P, KT, D], F32R)
        first_ctx, _ = place("first_ctx", [P, KT, D], F32, over=r1_hi_at)
        first_w0, _ = place("first_w0", [P, KT, D], F32, over=r1_lo_at)
        rt_hi, _ = place("rt_hi", [P, 2, KT, P], F32R)
        rt_lo, rt_lo_at = place("rt_lo", [P, 2, KT, P], F32R)
        q1_t = [place(f"q1_t{i}", [P, KT, P], BF16, over=rt_lo_at + i * KT * P * 4)[0] for i in range(2)]
        e_sb, e_at = place("e_sb", [P, TILES, D], F32)
        q2, _ = place("q2", [P, KT, D], BF16, over=e_at)
        rows, _ = place("rows", [P, 2, D], F32)
        q1, q1_at = place("q1", [P, 2, D], BF16)
        over_q1 = q1_at + D * 2
        lowt_hi, _ = place("lowt_hi", [P, P], F32R, over=over_q1)
        lowt_lo, _ = place("lowt_lo", [P, P], F32R, over=over_q1 + 512)
        low_s, _ = place("low_s", [P, ER], F32, over=over_q1 + 1024)
        raw, _ = place("raw", [P, RAW, D], F32)
        a_hi, _ = place("a_hi", [P, KT, ER + EXPERTS], F32R)
        a_lo, _ = place("a_lo", [P, KT, ER + EXPERTS], F32R)
        bb_hi, _ = place("bb_hi", [P, D], F32R)
        bb_lo, _ = place("bb_lo", [P, D], F32R)
        vec, _ = place("vec", [P, D], F32)
        ident, _ = place("ident", [P, P], F32)
        ident16, _ = place("ident16", [P, P], BF16)
        ones16, _ = place("ones16", [P, P], BF16)
        gate_raw, _ = place("gate_raw", [P, KT, EXPERTS], F32)
        low, _ = place("low", [P, ER + EXPERTS], F32)
        small, _ = place("small", [P, 112], F32)
        idx, _ = place("idx", [P, 8], U32)
        free = [0]

        def cols(n=1):
            free[0] += n
            assert free[0] <= 112
            return small[:, free[0] - n:free[0]]

        s1, z1, s2, z2 = scal = cols(), cols(), cols(), cols()
        inv_s1, inv_s2, s12 = cols(), cols(), cols()
        row_f, col_f, col_add, d2 = cols(), cols(), cols(), cols()
        stats, mv = cols(12), cols(2 * TILES)
        var_eps, rstd = cols(TILES), cols(TILES)
        minus_half, coef, coef_raw = cols(), cols(), cols()
        q1_sum, row_term = cols(TILES), cols(TILES)
        neg_max, e_sum, e_inv = cols(2), cols(TILES), cols(TILES)
        top, gap, gap_exp, gap_den, top_w, idx_f = cols(8), cols(), cols(), cols(), cols(TOP), cols(TOP)
        expert_no, one_hot, expert_w = cols(EXPERTS), cols(TOP * EXPERTS), cols(EXPERTS)

        acc = es.enter_context(nc.psum_tensor("acc", [P, 2, D], F32))
        tp = es.enter_context(nc.psum_tensor("tp", [P, 2, HALF], F32))
        low_ps = es.enter_context(nc.psum_tensor("low_ps", [P, HALF], F32))
        lowt_ps = es.enter_context(nc.psum_tensor("lowt_ps", [P, HALF], F32))

        sem = lambda name: es.enter_context(nc.semaphore(name))
        scalars_in = sem("scalars_in")
        x_in = [sem(f"x_in{t}") for t in range(TILES)]
        first_ctx_in = [sem(f"first_ctx_in{k}") for k in range(KT)]
        first_w0_in = [sem(f"first_w0_in{k}") for k in range(KT)]
        raw_in = [sem(f"raw_in{i}") for i in range(RAW)]
        gate_in = sem("gate_in")
        bias_in = sem("bias_in")
        out_done = [sem(f"out_done{t}") for t in range(TILES)]
        consts_ready = sem("consts_ready")
        pool_step = sem("pool_step")
        input_rstd_ready = sem("input_rstd_ready")
        rstd_ready = sem("rstd_ready")
        x_added = sem("x_added")
        dve_step = sem("dve_step")
        scalars_ready = sem("scalars_ready")
        input_var_ready = sem("input_var_ready")
        var_ready = sem("var_ready")
        rows_ready = sem("rows_ready")
        q1_rounded = sem("q1_rounded")
        row_term_ready = sem("row_term_ready")
        lo_done = sem("lo_done")
        first_lo = sem("first_lo")
        unit_lo = sem("unit_lo")
        gate_lo = sem("gate_lo")
        acc_free = sem("acc_free")
        col_term_ready = sem("col_term_ready")
        max_ready = sem("max_ready")
        gap_ready = sem("gap_ready")
        low_ready = sem("low_ready")
        lowt_lo_done = sem("lowt_lo_done")
        act_step = sem("act_step")
        first_hi = sem("first_hi")
        unit_hi = sem("unit_hi")
        gate_hi = sem("gate_hi")
        q1_ready = sem("q1_ready")
        x_row_added = sem("x_row_added")
        hi_done = sem("hi_done")
        exp_done = sem("exp_done")
        gap_exp_ready = sem("gap_exp_ready")
        lowt_hi_done = sem("lowt_hi_done")
        tr_done = sem("tr_done")
        acc_done = sem("acc_done")
        low_done = sem("low_done")
        lowt_done = sem("lowt_done")
        colsum_done = sem("colsum_done")

        dest = {"kt": (r1_hi, r1_lo), "v": (r0_hi, r0_lo), "w1": (r1_hi, r1_lo), "w0": (r0_hi, r0_lo)}

        def unit_dest(m, k):
            if m in dest:
                return dest[m][0][:, k, :], dest[m][1][:, k, :]
            if m in ("lora0a", "lora1a"):
                return a_hi[:, :, 0:ER], a_lo[:, :, 0:ER]
            return bb_hi[:, :], bb_lo[:, :]

        def unit_raw(u):
            m, slot = units[u][1], raw[:, u % RAW, :]
            if m in ("lora0a", "lora1a"):
                return slot.rearrange("p (k e) -> p k e", k=KT)
            return slot

        def unit_source(m, b, k):
            r = slice(k * P, (k + 1) * P)
            return {"kt": ctx_t[b, r, :], "v": ctx[b, r, :], "q2": ctx[b, r, :], "w1": w1_t[r, :], "w0": w0_t[r, :],
                    "lora0a": a0_t, "lora0b": bb0_t, "lora1a": a1_t, "lora1b": bb1_t}[m]

        def last_reader(m, b):
            if m in ("lora0a", "lora0b", "kt"):
                return job(b - 1, FFN1, TILES - 1) if b else None
            if m in ("v", "lora1a", "lora1b"):
                return job(b, FFN0, TILES - 1)
            if m == "w1":
                return job(b, QK, TILES - 1)
            return job(b - 1, PV, TILES - 1)

        block = es.enter_context(nc.Block())

        @block.sync
        def _(sp):
            for dst, src in zip(scal, q_scalars):
                sp.dma_start(dst, src.partition_broadcast(P)).then_inc(scalars_in, 16)
            sp.dma_start(coef_raw, lora_w).then_inc(scalars_in, 16)
            sp.dma_start(x_sb[:, 0, :], x[0, 0:P, :]).then_inc(x_in[0], 16)
            for k in range(KT):
                sp.dma_start(first_ctx[:, k, :], ctx[0, k * P:(k + 1) * P, :]).then_inc(first_ctx_in[k], 16)
            for t in range(1, TILES):
                sp.dma_start(x_sb[:, t, :], x[0, t * P:(t + 1) * P, :]).then_inc(x_in[t], 16)
            sp.dma_start(gate_raw[:, :, :], gate_t).then_inc(gate_in, 16)
            for k in range(KT):
                sp.dma_start(first_w0[:, k, :], w0_t[k * P:(k + 1) * P, :]).then_inc(first_w0_in[k], 16)
            for u, (_, m, b, k) in enumerate(units):
                if u >= RAW:
                    sp.wait_ge(unit_lo, u - RAW + 1)
                sp.dma_start(raw[:, u % RAW, :], unit_source(m, b, k)).then_inc(raw_in[u % RAW], 16)

        @block.gpsimd
        def _(pool):
            steps = [0]

            def own(ins):
                steps[0] += 1
                ins.then_inc(pool_step, 1)
                pool.wait_ge(pool_step, steps[0])

            own(nc.gpsimd.memset(ident[:, :], 0.0))
            own(nc.gpsimd.affine_select(out=ident[:, :], in_=ident[:, :], compare_op=ALU.not_equal, fill=1.0,
                                        base=0, pattern=[[-1, P]], channel_multiplier=1))
            nc.gpsimd.tensor_copy(ident16[:, :], ident[:, :])
            nc.gpsimd.memset(ones16[:, :], 1.0)
            nc.gpsimd.memset(minus_half, -0.5)
            for e in range(EXPERTS):
                last = nc.gpsimd.memset(expert_no[:, e:e + 1], float(e))
            own(last)
            nc.gpsimd.memset(top_w, 0.0).then_inc(consts_ready, 1)

            def inverse_deviation(n):
                _, s, t = stage_of(n)
                pool.wait_ge(input_var_ready if s == QMM else var_ready, norm_no(n) + 1)
                nc.gpsimd.tensor_tensor(out=rstd[:, t:t + 1], in0=var_eps[:, t:t + 1], in1=minus_half,
                                        op=ALU.pow).then_inc(input_rstd_ready if s == QMM else rstd_ready, 1)

            def add_vector(n):
                b, s, t = stage_of(n)
                if s == QMM:
                    pool.wait_ge(x_row_added, tile_no(n) + 1)
                    pool.wait_ge(col_term_ready, b + 1)
                else:
                    pool.wait_ge(rows_ready, row_no(n) + 1)
                    pool.wait_ge(bias_in, 16 * (2 * b + (1 if s == FFN0 else 2)))
                nc.gpsimd.tensor_tensor(out=x_sb[:, t, :], in0=x_sb[:, t, :], in1=vec[:, :],
                                        op=ALU.add).then_inc(x_added, 1)

            inverse_deviation(0)
            for n in range(-1, N):
                b, s, t = stage_of(n)
                if n >= 1 and stage_of(n - 1)[1] in (QMM, FFN0, PV):
                    inverse_deviation(n - 1 + TILES)
                nxt = n + 1
                if nxt < N and stage_of(nxt)[1] in (QMM, FFN0, FFN1):
                    add_vector(nxt)
                if n + 2 < N and n + 2 >= 1 and stage_of(n + 2)[1] == QMM:
                    inverse_deviation(n + 2)

        @block.vector
        def _(dve):
            steps = [0]

            def own(ins):
                steps[0] += 1
                ins.then_inc(dve_step, 1)
                dve.wait_ge(dve_step, steps[0])

            def norm_stats(n):
                _, s, t = stage_of(n)
                ready = input_var_ready if s == QMM else var_ready
                st = stats.rearrange("p (h c) -> p h c", h=2)
                nc.vector.bn_stats(out=st[:, 0, :], in_=x_sb[:, t, 0:HALF])
                own(nc.vector.bn_stats(out=st[:, 1, :], in_=x_sb[:, t, HALF:D]))
                own(nc.vector.bn_aggr(out=mv[:, 2 * t:2 * t + 2], in_=st))
                nc.vector.tensor_scalar(var_eps[:, t:t + 1], mv[:, 2 * t + 1:2 * t + 2], EPS, None,
                                        ALU.add).then_inc(ready, 1)
                dve.wait_ge(ready, norm_no(n) + 1)

            def round_q(dst, v):
                own(nc.vector.tensor_scalar(v, v, MAGIC, MAGIC, ALU.add, ALU.max))
                return nc.vector.tensor_scalar(dst, v, MAGIC + QMAX, MAGIC + MID, ALU.min, ALU.subtract)

            def make_rows(n):
                b, s, t = stage_of(n)
                dst = rows[:, n % 2, :]
                if n >= 2:
                    if stage_of(n - 2)[1] == QMM:
                        dve.wait_ge(q1_ready, tile_no(n - 2) + 1)
                    else:
                        dve.wait_ge(tr_done, 2 * (n - 2) + 2)
                if s == PV:
                    nc.vector.tensor_scalar(dst, e_sb[:, t, :], e_inv[:, t:t + 1], None,
                                            ALU.mult).then_inc(rows_ready, 1)
                    return
                dve.wait_ge(input_rstd_ready if s == QMM else rstd_ready, norm_no(n) + 1)
                normed = nc.vector.tensor_scalar(dst, x_sb[:, t, :], mv[:, 2 * t:2 * t + 1], rstd[:, t:t + 1],
                                                 ALU.subtract, ALU.mult)
                if s != QMM:
                    normed.then_inc(rows_ready, 1)
                    return
                own(normed)
                own(nc.vector.tensor_scalar(dst, dst, inv_s1, z1, ALU.mult, ALU.add))
                own(nc.vector.tensor_scalar(dst, dst, MAGIC, MAGIC, ALU.add, ALU.max))
                nc.vector.tensor_scalar(dst, dst, MAGIC + QMAX, None, ALU.min).then_inc(q1_rounded, 1)

            def finish_q1(n):
                t = stage_of(n)[2]
                dve.wait_ge(q1_ready, tile_no(n) + 1)
                nc.vector.tensor_scalar(row_term[:, t:t + 1], q1_sum[:, t:t + 1], row_f, None,
                                        ALU.mult).then_inc(row_term_ready, 1)

            def split_low_half(n):
                for h in range(2):
                    ks = slice(h * KH, (h + 1) * KH)
                    dve.wait_ge(hi_done, 2 * n + h + 1)
                    nc.vector.tensor_tensor(out=rt_lo[:, n % 2, ks, :],
                                            in0=tp[:, h, :].rearrange("p (k r) -> p k r", k=KH),
                                            in1=rt_hi[:, n % 2, ks, :].bitcast(F32),
                                            op=ALU.subtract).then_inc(lo_done, 1)

            def do_unit(u):
                _, m, b, k = units[u]
                src = unit_raw(u)
                dve.wait_ge(unit_hi, u + 1)
                if m == "q2":
                    round_q(q2[:, k, :], src).then_inc(unit_lo, 1)
                    return
                hi, lo = unit_dest(m, k)
                if m == "lora1b":
                    nc.vector.scalar_tensor_tensor(out=lo, in0=src, scalar=coef, in1=hi.bitcast(F32),
                                                   op0=ALU.mult, op1=ALU.subtract).then_inc(unit_lo, 1)
                else:
                    nc.vector.tensor_tensor(out=lo, in0=src, in1=hi.bitcast(F32), op=ALU.subtract).then_inc(unit_lo, 1)
                if m == "lora0a":
                    dve.wait_ge(gate_hi, b + 1)
                    nc.vector.tensor_tensor(out=a_lo[:, :, ER:], in0=gate_raw[:, :, :],
                                            in1=a_hi[:, :, ER:].bitcast(F32), op=ALU.subtract).then_inc(gate_lo, 1)

            def column_term(b):
                if b:
                    dve.wait_ge(x_added, add_no(job(b - 1, FFN1, TILES - 1)) + 1)
                dve.wait_ge(colsum_done, b + 1)
                nc.vector.tensor_scalar(vec[:, 0:HALF], low_ps[:, :], col_add, col_f, ALU.add, ALU.mult)
                nc.vector.tensor_scalar(vec[:, HALF:D], lowt_ps[:, :], col_add, col_f, ALU.add,
                                        ALU.mult).then_inc(col_term_ready, 1)

            def take_sums(n):
                b, s, t = stage_of(n)
                dve.wait_ge(acc_done, n + 1)
                a, xt = acc[:, n % 2, :], x_sb[:, t, :]
                if s == QK:
                    own(nc.vector.tensor_reduce(out=neg_max[:, 0:1], in_=a, axis=AX.X, op=ALU.max))
                    if tile_no(n):
                        dve.wait_ge(exp_done, tile_no(n))
                    nc.vector.tensor_scalar(neg_max[:, 1:2], neg_max[:, 0:1], -1.0, None,
                                            ALU.mult).then_inc(max_ready, 1)
                    return
                if s in (QMM, FFN0, FFN1):
                    dve.wait_ge(x_added, add_no(n) + 1)
                if s == QMM:
                    added = nc.vector.scalar_tensor_tensor(out=xt, in0=a, scalar=s12, in1=xt, op0=ALU.mult, op1=ALU.add)
                else:
                    added = nc.vector.tensor_tensor(out=xt, in0=a, in1=xt, op=ALU.add)
                added.then_inc(acc_free, 1)
                dve.wait_ge(acc_free, n + 1)
                if s != FFN1:
                    if s != QK:
                        norm_stats(n + TILES)

            def invert_sum(n):
                t = stage_of(n)[2]
                dve.wait_ge(exp_done, tile_no(n) + 1)
                nc.vector.reciprocal(e_inv[:, t:t + 1], e_sum[:, t:t + 1]).then_inc(acc_free, 1)
                dve.wait_ge(acc_free, n + 1)

            def low_rank(n):
                b, s, t = stage_of(n)
                dve.wait_ge(low_done, lora_no(n) + 1)
                if n and lora_no(n):
                    dve.wait_ge(lowt_done, lora_no(n))
                if s == FFN1:
                    nc.vector.tensor_copy(low_s[:, :], low_ps[:, 0:ER]).then_inc(low_ready, 1)
                    return
                own(nc.vector.tensor_copy(low[:, :], low_ps[:, 0:ER + EXPERTS]))
                logits = low[:, ER:]
                own(nc.vector.max(out=top, in_=logits))
                nc.vector.max_index(out=idx[:, :], in_max=top, in_values=logits)
                nc.vector.tensor_tensor(out=gap, in0=top[:, 1:2], in1=top[:, 0:1], op=ALU.subtract).then_inc(gap_ready, 1)
                dve.wait_ge(gap_ready, TILES * b + t + 1)
                own(nc.vector.tensor_copy(idx_f, idx[:, 0:TOP]))
                dve.wait_ge(gap_exp_ready, TILES * b + t + 1)
                own(nc.vector.tensor_scalar(gap_den, gap_exp, 1.0, None, ALU.add))
                own(nc.vector.reciprocal(top_w[:, 0:1], gap_den))
                own(nc.vector.tensor_tensor(out=top_w[:, 1:2], in0=gap_exp, in1=top_w[:, 0:1], op=ALU.mult))
                for i in range(TOP):
                    oh = nc.vector.tensor_scalar(one_hot[:, i * EXPERTS:(i + 1) * EXPERTS], expert_no,
                                                 idx_f[:, i:i + 1], top_w[:, i:i + 1], ALU.is_equal, ALU.mult)
                own(oh)
                own(nc.vector.tensor_tensor(out=expert_w, in0=one_hot[:, 0:EXPERTS], in1=one_hot[:, EXPERTS:], op=ALU.add))
                nc.vector.scalar_tensor_tensor(
                    out=low_s[:, :].rearrange("p (e r) -> p e r", e=EXPERTS),
                    in0=low[:, 0:ER].rearrange("p (e r) -> p e r", e=EXPERTS), scalar=SCALING,
                    in1=expert_w.unsqueeze(2).to_broadcast([P, EXPERTS, RANK]),
                    op0=ALU.mult, op1=ALU.mult).then_inc(low_ready, 1)

            def split_low_rank(n):
                dve.wait_ge(lowt_hi_done, lora_no(n) + 1)
                nc.vector.tensor_tensor(out=lowt_lo[:, :], in0=lowt_ps[:, 0:P], in1=lowt_hi[:, :].bitcast(F32),
                                        op=ALU.subtract).then_inc(lowt_lo_done, 1)

            dve.wait_ge(scalars_in, 16 * 5)
            nc.vector.reciprocal(inv_s1, s1)
            nc.vector.reciprocal(inv_s2, s2)
            nc.vector.tensor_scalar(coef, coef_raw, SCALING, None, ALU.mult)
            nc.vector.tensor_scalar(d2, z2, -1.0, MID, ALU.mult, ALU.add)
            nc.vector.tensor_scalar(col_f, z1, -1.0, MID, ALU.mult, ALU.add)
            own(nc.vector.tensor_tensor(out=s12, in0=s1, in1=s2, op=ALU.mult))
            nc.vector.tensor_tensor(out=row_f, in0=s12, in1=d2, op=ALU.mult)
            nc.vector.tensor_tensor(out=col_f, in0=s12, in1=col_f, op=ALU.mult)
            nc.vector.tensor_scalar(col_add, d2, float(D), None, ALU.mult).then_inc(scalars_ready, 1)
            dve.wait_ge(scalars_ready, 1)
            dve.wait_ge(x_in[0], 16)
            norm_stats(0)
            dve.wait_ge(consts_ready, 1)
            make_rows(0)
            for k in range(KT):
                dve.wait_ge(first_hi, k + 1)
                round_q(q2[:, k, :], first_ctx[:, k, :]).then_inc(first_lo, 1)
            finish_q1(0)
            dve.wait_ge(x_in[1], 16)
            norm_stats(1)
            column_term(0)
            for k in range(KT):
                if k == 2:
                    make_rows(1)
                if k == 4:
                    finish_q1(1)
                dve.wait_ge(first_hi, KT + k + 1)
                nc.vector.tensor_tensor(out=r0_lo[:, k, :], in0=first_w0[:, k, :], in1=r0_hi[:, k, :].bitcast(F32),
                                        op=ALU.subtract).then_inc(first_lo, 1)
            for n in range(N):
                b, s, t = stage_of(n)
                nxt = n + 1
                todo = list(window_units[n])
                if n:
                    take_sums(n - 1)
                if nxt < N and nxt > 1:
                    make_rows(nxt)
                if todo:
                    do_unit(todo.pop(0))
                if has_lora(s):
                    low_rank(n)
                if nxt < N and stage_of(nxt)[1] == QMM and nxt > 1:
                    finish_q1(nxt)
                if n and stage_of(n - 1)[1] == QK:
                    invert_sum(n - 1)
                if len(todo) > 1:
                    do_unit(todo.pop(0))
                if nxt < N and stage_of(nxt)[1] != QMM:
                    split_low_half(nxt)
                if has_lora(s):
                    split_low_rank(n)
                for u in todo:
                    do_unit(u)
                if nxt == JOBS * (b + 1) and nxt < N:
                    column_term(b + 1)
                after = n + 2
                if after < N and stage_of(after)[1] == QMM:
                    ab, _, atile = stage_of(after)
                    dve.wait_ge(x_in[atile], 16 * (ab + 1))
                    norm_stats(after)
            take_sums(N - 1)

        @block.scalar
        def _(act):
            steps = [0]

            def finish_q1(n):
                t = stage_of(n)[2]
                act.wait_ge(q1_rounded, tile_no(n) + 1)
                if n > 1:
                    act.wait_ge(acc_done, n - 1)
                nc.scalar.activation(q1[:, n % 2, :], rows[:, n % 2, :], ACT.Copy, bias=-(MAGIC + MID),
                                     accum_out=q1_sum[:, t:t + 1]).then_inc(q1_ready, 1)

            def add_row_term(n):
                t = stage_of(n)[2]
                act.wait_ge(row_term_ready, tile_no(n) + 1)
                nc.scalar.activation(x_sb[:, t, :], x_sb[:, t, :], ACT.Identity,
                                     bias=row_term[:, t:t + 1]).then_inc(x_row_added, 1)

            def split_high_half(n):
                s = stage_of(n)[1]
                for h in range(2):
                    ks = slice(h * KH, (h + 1) * KH)
                    act.wait_ge(tr_done, 2 * n + h + 1)
                    if s == QMM:
                        src = tp[:, h, 0:HALF // 2].bitcast(BF16).rearrange("p (k r) -> p k r", k=KH)
                        dst = q1_t[n % 2][:, ks, :]
                    else:
                        src = tp[:, h, :].rearrange("p (k r) -> p k r", k=KH)
                        dst = rt_hi[:, n % 2, ks, :]
                    nc.scalar.activation(dst, src, ACT.Copy).then_inc(hi_done, 1)

            def do_unit(u):
                _, m, b, k = units[u]
                src = unit_raw(u)
                act.wait_ge(raw_in[u % RAW], 16 * (u // RAW + 1))
                reader = last_reader(m, b)
                if reader is not None:
                    act.wait_ge(acc_done, reader + 1)
                if m == "kt" and b == 0:
                    act.wait_ge(first_lo, 2 * KT)
                if m == "q2":
                    nc.scalar.activation(src, src, ACT.Identity, bias=z2, scale=inv_s2).then_inc(unit_hi, 1)
                    return
                hi, _ = unit_dest(m, k)
                scale = coef if m == "lora1b" else 1.0
                nc.scalar.activation(hi, src, ACT.Copy, scale=scale).then_inc(unit_hi, 1)
                if m == "lora0a":
                    act.wait_ge(gate_in, 16)
                    nc.scalar.activation(a_hi[:, :, ER:], gate_raw[:, :, :], ACT.Copy).then_inc(gate_hi, 1)

            def exponentials(n):
                t = stage_of(n)[2]
                act.wait_ge(max_ready, tile_no(n) + 1)
                nc.scalar.activation(e_sb[:, t, :], acc[:, n % 2, :], ACT.Exp, bias=neg_max[:, 1:2],
                                     accum_out=e_sum[:, t:t + 1]).then_inc(exp_done, 1)

            def load_bias(b, s):
                act.wait_ge(x_added, add_no(job(b, QMM if s == FFN0 else FFN0, TILES - 1)) + 1)
                act.dma_start(vec[:, :], (b0 if s == FFN0 else b1).partition_broadcast(P)).then_inc(bias_in, 16)

            act.wait_ge(scalars_ready, 1)
            for k in range(KT):
                if k == 2:
                    act.wait_ge(q1_rounded, 1)
                    nc.scalar.activation(q1[:, 0, :], rows[:, 0, :], ACT.Copy, bias=-(MAGIC + MID),
                                         accum_out=q1_sum[:, 0:1]).then_inc(q1_ready, 1)
                if k == 4:
                    split_high_half(0)
                act.wait_ge(first_ctx_in[k], 16)
                nc.scalar.activation(first_ctx[:, k, :], first_ctx[:, k, :], ACT.Identity, bias=z2,
                                     scale=inv_s2).then_inc(first_hi, 1)
            add_row_term(0)
            for k in range(KT):
                if k == 3:
                    finish_q1(1)
                if k == 6:
                    add_row_term(1)
                act.wait_ge(first_w0_in[k], 16)
                nc.scalar.activation(r0_hi[:, k, :], first_w0[:, k, :], ACT.Copy).then_inc(first_hi, 1)
            for n in range(N):
                b, s, t = stage_of(n)
                nxt = n + 1
                todo = list(window_units[n])
                if n and stage_of(n - 1)[1] == QK:
                    exponentials(n - 1)
                if nxt < N and stage_of(nxt)[1] == QMM and nxt > 1:
                    finish_q1(nxt)
                if n and stage_of(n - 1)[1] == FFN1:
                    ob, _, ot = stage_of(n - 1)
                    act.wait_ge(acc_free, n)
                    act.dma_start(out[ob, ot * P:(ot + 1) * P, :], x_sb[:, ot, :]).then_inc(out_done[ot], 16)
                if todo:
                    do_unit(todo.pop(0))
                if s == FFN0:
                    act.wait_ge(gap_ready, tile_no(n) + 1)
                    nc.scalar.activation(gap_exp, gap, ACT.Exp).then_inc(gap_exp_ready, 1)
                if len(todo) > 1:
                    do_unit(todo.pop(0))
                if nxt < N:
                    split_high_half(nxt)
                if nxt < N and stage_of(nxt)[1] == QMM and nxt > 1:
                    add_row_term(nxt)
                if n >= 2 and stage_of(n - 2)[1] == FFN1 and stage_of(n - 2)[0] + 1 < BATCHES:
                    ob, _, ot = stage_of(n - 2)
                    act.wait_ge(out_done[ot], 16 * (ob + 1))
                    act.dma_start(x_sb[:, ot, :], x[ob + 1, ot * P:(ot + 1) * P, :]).then_inc(x_in[ot], 16)
                if s == QMM and t == TILES - 1:
                    load_bias(b, FFN0)
                if s == QK and t == 0:
                    load_bias(b, FFN1)
                if has_lora(s):
                    act.wait_ge(lowt_done, lora_no(n) + 1)
                    if n and lora_no(n):
                        act.wait_ge(acc_done, n)
                    nc.scalar.activation(lowt_hi[:, :], lowt_ps[:, 0:P], ACT.Copy).then_inc(lowt_hi_done, 1)
                for u in todo:
                    do_unit(u)
            act.wait_ge(acc_free, N)
            act.dma_start(out[BATCHES - 1, ROWS - P:ROWS, :], x_sb[:, TILES - 1, :]).then_inc(out_done[TILES - 1], 16)
            for t in range(TILES):
                act.wait_ge(out_done[t], 16 * BATCHES)

        @block.tensor
        def _(pe):
            def transposes(n):
                s = stage_of(n)[1]
                if s == QMM:
                    pe.wait_ge(q1_ready, tile_no(n) + 1)
                else:
                    pe.wait_ge(rows_ready, row_no(n) + 1)
                for h in range(2):
                    for i in range(KH):
                        k = h * KH + i
                        if s == QMM:
                            dst = tp[:, h, 0:HALF // 2].bitcast(BF16)[:, i * P:(i + 1) * P]
                            last = nc.tensor.transpose(dst, q1[:, n % 2, k * P:(k + 1) * P], ident16[:, :])
                        else:
                            last = nc.tensor.transpose(tp[:, h, i * P:(i + 1) * P],
                                                       rows[:, n % 2, k * P:(k + 1) * P], ident[:, :])
                    last.then_inc(tr_done, 1)

            def matrix_ready(s, b, k):
                if s == FFN0 and b == 0:
                    pe.wait_ge(first_lo, KT + k + 1)
                elif s == QMM and b == 0:
                    pe.wait_ge(first_lo, k + 1)
                else:
                    m = {QMM: "q2", FFN0: "w0", QK: "kt", PV: "v", FFN1: "w1"}[s]
                    pe.wait_ge(unit_lo, unit_no[m, b, k] + 1)

            def rows_split(n, h):
                if stage_of(n)[1] == QMM:
                    pe.wait_ge(hi_done, 2 * n + h + 1)
                else:
                    pe.wait_ge(lo_done, 2 * row_no(n) + h + 1)

            def column_sums(b):
                for h, dst in enumerate((low_ps, lowt_ps)):
                    for k in range(KT):
                        if h == 0:
                            matrix_ready(QMM, b, k)
                        last = nc.tensor.matmul(dst[:, :], ones16[:, :], q2[:, k, h * HALF:(h + 1) * HALF],
                                                start=(k == 0), stop=(k == KT - 1))
                last.then_inc(colsum_done, 1)

            PASSES = ((0, 0), (0, 1), (1, 0))

            pe.wait_ge(consts_ready, 1)
            transposes(0)
            column_sums(0)
            for n in range(N):
                b, s, t = stage_of(n)
                p = n % 2
                left = (rt_hi, rt_lo)
                right = {FFN0: (r0_hi, r0_lo), QK: (r1_hi, r1_lo), PV: (r0_hi, r0_lo), FFN1: (r1_hi, r1_lo)}.get(s)
                lora_left, lora_right = (a_hi, a_lo), (bb_hi, bb_lo)
                rows_split(n, 0)
                if n >= 2:
                    pe.wait_ge(acc_free, n - 1)
                if has_lora(s):
                    rows_split(n, 1)
                    if t == 0:
                        m = "lora0" if s == FFN0 else "lora1"
                        pe.wait_ge(unit_lo, unit_no[m + "a", b, 0] + 1)
                        pe.wait_ge(unit_lo, unit_no[m + "b", b, 0] + 1)
                        pe.wait_ge(gate_lo, b + 1)
                    if t == 0 and s == FFN0:
                        pe.wait_ge(col_term_ready, b + 1)
                    width = ER + EXPERTS if s == FFN0 else ER
                    if lora_no(n):
                        pe.wait_ge(low_ready, lora_no(n))
                    for k in range(KT):
                        for i, (l, r) in enumerate(PASSES):
                            last = nc.tensor.matmul(low_ps[:, 0:width], left[l][:, p, k, :], lora_left[r][:, k, 0:width],
                                                    start=(k == 0 and i == 0), stop=(k == KT - 1 and i == 2))
                    last.then_inc(low_done, 1)
                for k in range(KT):
                    if k == KH:
                        rows_split(n, 1)
                        if n + 1 < N:
                            transposes(n + 1)
                    if t == 0:
                        matrix_ready(s, b, k)
                    end = k == KT - 1 and not has_lora(s)
                    if s == QMM:
                        for h in range(2):
                            last = nc.tensor.matmul(acc[:, p, h * HALF:(h + 1) * HALF], q1_t[p][:, k, :],
                                                    q2[:, k, h * HALF:(h + 1) * HALF], start=(k == 0), stop=end)
                        continue
                    for i, (l, r) in enumerate(PASSES):
                        for h in range(2):
                            last = nc.tensor.matmul(acc[:, p, h * HALF:(h + 1) * HALF], left[l][:, p, k, :],
                                                    right[r][:, k, h * HALF:(h + 1) * HALF],
                                                    start=(k == 0 and i == 0), stop=(end and i == 2))
                    if has_lora(s) and k == KT - 2:
                        pe.wait_ge(low_ready, lora_no(n) + 1)
                        nc.tensor.transpose(lowt_ps[:, 0:P], low_s[:, :], ident[:, :]).then_inc(lowt_done, 1)
                if has_lora(s):
                    pe.wait_ge(lowt_lo_done, lora_no(n) + 1)
                    lt = (lowt_hi, lowt_lo)
                    for i, (l, r) in enumerate(PASSES):
                        for h in range(2):
                            last = nc.tensor.matmul(acc[:, p, h * HALF:(h + 1) * HALF], lt[l][:, :],
                                                    lora_right[r][:, h * HALF:(h + 1) * HALF], start=False, stop=(i == 2))
                last.then_inc(acc_done, 1)
                if n + 1 < N and stage_of(n + 1)[1] == QMM and stage_of(n + 1)[2] == 0:
                    column_sums(b + 1)


def kernel(x, ctx_4096, L0_xattn_x1_scale, L0_xattn_x1_zp, L0_xattn_x2_scale, L0_xattn_x2_zp, L0_ffn_gate_w,
           L0_ffn_base_w, L0_ffn_base_b, L0_ffn_lora_A, L0_ffn_lora_B, L1_ffn_lora_A, L1_ffn_lora_B, L1_ffn_W,
           L1_ffn_bias, L1_ffn_lora_weights):
    import numpy as np
    import concourse.bacc as bacc
    from concourse.bass_utils import run_bass_kernel_spmd

    P = 128
    c = np.ascontiguousarray

    def k_tiles(m):
        m = np.asarray(m)
        return c(m.reshape(-1, P, m.shape[1]).transpose(1, 0, 2).reshape(P, -1))

    lora_a_t = lambda a: k_tiles(np.asarray(a).reshape(-1, a.shape[2]).T)
    lora_b_t = lambda a: c(np.asarray(a).transpose(0, 2, 1).reshape(-1, a.shape[1]))
    rank = L1_ffn_lora_A.shape[1]
    arrays = {
        "x": c(x), "ctx": c(ctx_4096), "ctx_t": c(np.asarray(ctx_4096).transpose(0, 2, 1)),
        "s1": c(L0_xattn_x1_scale), "z1": c(L0_xattn_x1_zp), "s2": c(L0_xattn_x2_scale), "z2": c(L0_xattn_x2_zp),
        "gate_t": k_tiles(np.asarray(L0_ffn_gate_w).T), "w0_t": c(np.asarray(L0_ffn_base_w).T), "b0": c(L0_ffn_base_b),
        "a0_t": lora_a_t(L0_ffn_lora_A), "bb0_t": lora_b_t(L0_ffn_lora_B),
        "a1_t": lora_a_t(L1_ffn_lora_A), "bb1_t": lora_b_t(L1_ffn_lora_B),
        "w1_t": c(np.asarray(L1_ffn_W).T), "b1": c(L1_ffn_bias),
        "lora_w": c(np.repeat(np.asarray(L1_ffn_lora_weights), rank).reshape(-1, 1)),
    }
    nc = bacc.Bacc("TRN2", target_bir_lowering=False, num_devices=1, dynamic_dma_scratch_size=1024)
    dram = {n: nc.dram_tensor(n, a.shape, mybir.dt.from_np(a.dtype), kind="ExternalInput").ap() for n, a in arrays.items()}
    out = nc.dram_tensor("out", arrays["x"].shape, mybir.dt.float32, kind="ExternalOutput").ap()
    g = dram["gate_t"].rearrange("p (k e) -> p k e", e=L0_ffn_gate_w.shape[0])
    two_layer_kernel(nc, dram["x"], dram["ctx"], dram["ctx_t"], [dram[n] for n in ("s1", "z1", "s2", "z2")], g,
                     dram["w0_t"], dram["b0"], dram["a0_t"], dram["bb0_t"], dram["a1_t"], dram["bb1_t"], dram["w1_t"],
                     dram["b1"], dram["lora_w"], out)
    got = run_bass_kernel_spmd(nc, [arrays], core_ids=[0])
    return got.results[0]["out"]
```

```python
from concourse import mybir
from contextlib import ExitStack

F32 = mybir.dt.float32
F32R = mybir.dt.float32r
BF16 = mybir.dt.bfloat16
U32 = mybir.dt.uint32
ALU = mybir.AluOpType
ACT = mybir.ActivationFunctionType
AX = mybir.AxisListType


def two_layer_kernel(nc, x, ctx, ctx_t, q_scalars, gate_t, w0_t, b0, a0_t, bb0_t, a1, bb1_t, w1_t, b1, lora_w, out):
    P = nc.NUM_PARTITIONS
    BATCHES, ROWS, D = x.shape
    KT = D // P
    TILES = ROWS // P
    HALF = D // 2
    KH = KT // 2
    EXPERTS, RANK = 8, 16
    ER = EXPERTS * RANK
    LOW = ER + EXPERTS
    TOP = 2
    SCALING = 2.0
    EPS = 1e-5
    QMAX = 255.0
    MID = 128.0
    MAGIC = 12582912.0
    QMM, FFN0, QK, PV, FFN1 = STAGES = range(5)
    JOBS = len(STAGES) * TILES
    RAW = 3

    SEQ = []
    for b in range(BATCHES):
        first = [(b, QMM, 0), (b, QMM, 1), (b, QMM, 2), (b, FFN0, 0), (b, QMM, 3), (b, FFN0, 1), (b, FFN0, 2), (b, FFN0, 3)]
        if b:
            first = [(b, QMM, 0), SEQ.pop(), (b, QMM, 1), (b, FFN0, 0), (b, QMM, 2), (b, FFN0, 1), (b, QMM, 3),
                     (b, FFN0, 2), (b, FFN0, 3)]
        SEQ += first + [(b, s, t) for s in (QK, PV, FFN1) for t in range(TILES)]
    N = len(SEQ)
    POS = {j: n for n, j in enumerate(SEQ)}

    def rank(*stages):
        of = [n for n in range(N) if SEQ[n][1] in stages]
        return {n: i for i, n in enumerate(of)}

    nth = {s: rank(s) for s in STAGES}
    nth_float = rank(FFN0, QK, PV, FFN1)
    nth_added = rank(QMM, FFN0, FFN1)
    nth_normed = rank(QMM, FFN0, PV)
    NEXT_NORM = {QMM: FFN0, FFN0: QK, PV: FFN1}
    PREV_SUM = {v: k for k, v in NEXT_NORM.items()}

    def norm_no(n):
        b, s, t = SEQ[n]
        return nth[QMM][n] if s == QMM else nth_normed[POS[b, PREV_SUM[s], t]]

    LOAD_X = {POS[j]: (b, t) for b in range(1, BATCHES) for t, j in enumerate(
        [(b - 1, FFN1, 1), (b - 1, FFN1, 2), (b - 1, FFN1, 3), (b, FFN0, 0)])}
    NORM_X = {POS[j]: (b, t) for b in range(1, BATCHES) for t, j in enumerate(
        [(b - 1, FFN1, 1), (b - 1, FFN1, 2), (b, QMM, 1), (b, QMM, 2)])}
    NORM_X |= {POS[0, QMM, 2]: (0, 3)}

    is_quant = lambda n: 0 <= n < N and SEQ[n][1] == QMM
    MAKE_FIRST = [n + 1 if n + 1 < N and not is_quant(n) else None for n in range(N)]
    MAKE_LAST = [n + 2 if n + 2 < N and is_quant(n + 1) else None for n in range(N)]
    TRANSPOSE_AT = [KT - 2 if n == 0 else 0 if is_quant(n) else KH for n in range(N)]

    LOAD_BIAS = {POS[j]: (b, s) for b in range(BATCHES) for s, j in ((FFN0, (b, QMM, 1)), (FFN1, (b, QK, 0)))}

    def lot(m, b, first, count):
        return [(m, b, k) for k in range(first, first + count)]

    window_units = {n: [] for n in range(N)}
    first_units = {POS[0, QMM, 0]: [0], POS[0, QMM, 1]: [1], POS[0, QMM, 2]: [2], POS[0, FFN0, 0]: [3, 4, 5, 6, 7]}
    for b in range(BATCHES):
        plan = [((b, QMM, 1), [("lora0a", b, 0), ("lora0b", b, 0)]),
                ((b, FFN0, 1), lot("kt", b, 0, 3)), ((b, FFN0, 2), lot("kt", b, 3, 3)), ((b, FFN0, 3), lot("kt", b, 6, 2)),
                ((b, QK, 0), lot("v", b, 0, 3)), ((b, QK, 1), lot("v", b, 3, 3)), ((b, QK, 2), lot("v", b, 6, 2)),
                ((b, QK, 3), [("lora1a", b, 0), ("lora1b", b, 0)] if b == 0 else []),
                ((b, PV, 0), lot("w1", b, 0, 3)), ((b, PV, 1), lot("w1", b, 3, 3)), ((b, PV, 2), lot("w1", b, 6, 2))]
        if b + 1 < BATCHES:
            plan += [((b, PV, 3), lot("q2", b + 1, 0, 2)), ((b, FFN1, 0), lot("q2", b + 1, 2, 4)),
                     ((b, FFN1, 1), lot("q2", b + 1, 6, 2) + lot("w0", b + 1, 0, 2)),
                     ((b, FFN1, 2), lot("w0", b + 1, 2, 3)), ((b, FFN1, 3), lot("w0", b + 1, 5, 3))]
        for j, lots in plan:
            window_units[POS[j]] += lots
    units = [u for n in range(N) for u in window_units[n]]
    unit_no = {u: i for i, u in enumerate(units)}

    es = ExitStack()
    with es:
        at = [(nc.sbuf_base + 31) // 32 * 32]
        size = {F32: 4, F32R: 4, BF16: 2, U32: 4}

        def place(name, shape, dt, over=None):
            if over is None:
                over = at[0]
                n = size[dt]
                for d in shape[1:]:
                    n *= d
                at[0] += (n + 31) // 32 * 32
            return nc.alloc_sbuf_tensor_at(name, shape, dt, offset=over), over

        x_sb, _ = place("x_sb", [P, TILES, D], F32)
        r0_hi, _ = place("r0_hi", [P, KT, D], F32R)
        r0_lo, _ = place("r0_lo", [P, KT, D], F32R)
        r1_hi, r1_hi_at = place("r1_hi", [P, KT, D], F32R)
        r1_lo, r1_lo_at = place("r1_lo", [P, KT, D], F32R)
        first_ctx, _ = place("first_ctx", [P, KT, D], F32, over=r1_hi_at)
        first_w0, _ = place("first_w0", [P, KT, D], F32, over=r1_lo_at)
        rt_hi, _ = place("rt_hi", [P, 2, KT, P], F32R)
        rt_lo, rt_lo_at = place("rt_lo", [P, 2, KT, P], F32R)
        q1_t = [place(f"q1_t{i}", [P, KT, P], BF16, over=rt_lo_at + i * KT * P * 4)[0] for i in range(2)]
        e_sb, e_at = place("e_sb", [P, TILES, D], F32)
        q2, _ = place("q2", [P, KT, D], BF16, over=e_at)
        rows, _ = place("rows", [P, D], F32)
        q1, _ = place("q1", [P, D], BF16)
        lowt_hi, _ = place("lowt_hi", [P, P], F32R)
        lowt_lo, _ = place("lowt_lo", [P, P], F32R)
        low_s, _ = place("low_s", [P, ER], F32)
        raw, _ = place("raw", [P, RAW, D], F32)
        a_parts, _ = place("a_parts", [P, KT, 2, LOW], F32R)
        bb_hi, _ = place("bb_hi", [P, D], F32R)
        bb_lo, _ = place("bb_lo", [P, D], F32R)
        col_term, _ = place("col_term", [P, D], F32)
        bias, _ = place("bias", [P, D], F32)
        ident, _ = place("ident", [P, P], F32)
        ident16, _ = place("ident16", [P, P], BF16)
        ones16, _ = place("ones16", [P, P], BF16)
        gate_raw, _ = place("gate_raw", [P, KT, EXPERTS], F32)
        low, _ = place("low", [P, LOW], F32)
        small, _ = place("small", [P, 112], F32)
        idx, _ = place("idx", [P, 8], U32)
        free = [0]

        def cols(n=1):
            free[0] += n
            assert free[0] <= 112
            return small[:, free[0] - n:free[0]]

        scalars = cols(4)
        s1, z1, s2, z2 = (scalars[:, i:i + 1] for i in range(4))
        inv_s1, inv_s2, s12 = cols(), cols(), cols()
        row_f, col_f, col_add, d2 = cols(), cols(), cols(), cols()
        stats, mv = cols(12), cols(2 * TILES)
        var_eps, rstd = cols(TILES), cols(TILES)
        minus_half, coef, coef_raw = cols(), cols(), cols()
        q_scale, q_shift, q_mean, row_term = cols(), cols(), cols(), cols(TILES)
        neg_max, e_sum, e_inv = cols(2), cols(TILES), cols(TILES)
        top, gap, gap_exp, gap_den, top_w, idx_f = cols(8), cols(), cols(), cols(), cols(TOP), cols(TOP)
        expert_no, one_hot, expert_w = cols(EXPERTS), cols(TOP * EXPERTS), cols(EXPERTS)

        acc = es.enter_context(nc.psum_tensor("acc", [P, 2, D], F32))
        tp = es.enter_context(nc.psum_tensor("tp", [P, 2, HALF], F32))
        low_ps = es.enter_context(nc.psum_tensor("low_ps", [P, HALF], F32))
        lowt_ps = es.enter_context(nc.psum_tensor("lowt_ps", [P, HALF], F32))

        sem = lambda name: es.enter_context(nc.semaphore(name))
        scalars_in = sem("scalars_in")
        x_in = [sem(f"x_in{t}") for t in range(TILES)]
        first_ctx_in = [sem(f"first_ctx_in{k}") for k in range(KT)]
        first_w0_in = [sem(f"first_w0_in{k}") for k in range(KT)]
        raw_in = [sem(f"raw_in{i}") for i in range(RAW)]
        coef_in = sem("coef_in")
        folded_stored = [sem(f"folded_stored{i}") for i in range(RAW)]
        gate_in = sem("gate_in")
        bias_in = sem("bias_in")
        out_done = [sem(f"out_done{t}") for t in range(TILES)]
        consts_ready = sem("consts_ready")
        pool_step = sem("pool_step")
        input_rstd_ready = sem("input_rstd_ready")
        rstd_ready = sem("rstd_ready")
        x_added = sem("x_added")
        dve_step = sem("dve_step")
        scalars_ready = sem("scalars_ready")
        coef_ready = sem("coef_ready")
        input_var_ready = sem("input_var_ready")
        var_ready = sem("var_ready")
        rows_ready = sem("rows_ready")
        q1_ready = sem("q1_ready")
        lo_done = sem("lo_done")
        first_lo = sem("first_lo")
        unit_lo = sem("unit_lo")
        folded = sem("folded")
        gate_lo = sem("gate_lo")
        acc_free = sem("acc_free")
        col_term_ready = sem("col_term_ready")
        max_ready = sem("max_ready")
        gap_ready = sem("gap_ready")
        low_ready = sem("low_ready")
        lowt_lo_done = sem("lowt_lo_done")
        table_loaded = sem("table_loaded")
        first_hi = sem("first_hi")
        unit_hi = sem("unit_hi")
        gate_hi = sem("gate_hi")
        y1_ready = sem("y1_ready")
        row_term_ready = sem("row_term_ready")
        x_row_added = sem("x_row_added")
        hi_done = sem("hi_done")
        exp_done = sem("exp_done")
        gap_exp_ready = sem("gap_exp_ready")
        lowt_hi_done = sem("lowt_hi_done")
        tr_done = sem("tr_done")
        acc_done = sem("acc_done")
        low_done = sem("low_done")
        lowt_done = sem("lowt_done")
        colsum_done = sem("colsum_done")
        fold_done = sem("fold_done")

        dest = {"kt": (r1_hi, r1_lo), "v": (r0_hi, r0_lo), "w1": (r1_hi, r1_lo), "w0": (r0_hi, r0_lo)}

        def unit_dest(m, k):
            if m in dest:
                return dest[m][0][:, k, :], dest[m][1][:, k, :]
            if m in ("lora0a", "lora1a"):
                return a_parts[:, :, 0, 0:ER], a_parts[:, :, 1, 0:ER]
            return bb_hi[:, :], bb_lo[:, :]

        def unit_raw(u):
            m, slot = units[u][0], raw[:, u % RAW, :]
            if m in ("lora0a", "lora1a"):
                return slot.rearrange("p (k e) -> p k e", k=KT)
            return slot

        w1_folded = nc.dram_tensor("w1_folded", [D, D], F32).ap()

        def folds(m, b):
            return m == "w1" and b == 0

        def stored_count(k):
            slot = [unit_no["w1", 0, i] % RAW for i in range(k + 1)]
            return 16 * slot.count(slot[k])

        def unit_source(m, b, k):
            r = slice(k * P, (k + 1) * P)
            if m == "w1" and b:
                return w1_folded[r, :]
            return {"kt": ctx_t[b, r, :], "v": ctx[b, r, :], "q2": ctx[b, r, :], "w1": w1_t[r, :], "w0": w0_t[r, :],
                    "lora0a": a0_t, "lora0b": bb0_t, "lora1a": a1, "lora1b": bb1_t}[m]

        def last_reader(m, b):
            last = TILES - 1
            if m in ("lora0a", "lora0b", "kt"):
                return POS[b - 1, FFN1, last] if b else None
            if m in ("v", "lora1a", "lora1b"):
                return POS[b, FFN0, last]
            if m == "w1":
                return POS[b, QK, last]
            return POS[b - 1, PV, last] if m == "w0" else None

        block = es.enter_context(nc.Block())

        @block.sync
        def _(sp):
            def load_x(t):
                sp.dma_start(x_sb[:, t, :], x[0, t * P:(t + 1) * P, :]).then_inc(x_in[t], 16)

            sp.dma_start(scalars, q_scalars.partition_broadcast(P)).then_inc(scalars_in, 16)
            load_x(0)
            for k in range(KT):
                sp.dma_start(first_ctx[:, k, :], ctx[0, k * P:(k + 1) * P, :]).then_inc(first_ctx_in[k], 16)
                if k == KH - 1:
                    load_x(1)
            load_x(2)
            for k in range(KH):
                sp.dma_start(first_w0[:, k, :], w0_t[k * P:(k + 1) * P, :]).then_inc(first_w0_in[k], 16)
            sp.dma_start(coef_raw, lora_w).then_inc(coef_in, 16)
            sp.dma_start(gate_raw[:, :, :], gate_t).then_inc(gate_in, 16)
            for u in range(2):
                m, b, k = units[u]
                sp.dma_start(raw[:, u % RAW, :], unit_source(m, b, k)).then_inc(raw_in[u % RAW], 16)
            load_x(3)
            for k in range(KH, KT):
                sp.dma_start(first_w0[:, k, :], w0_t[k * P:(k + 1) * P, :]).then_inc(first_w0_in[k], 16)
            for u, (m, b, k) in enumerate(units[2:], 2):
                if u >= RAW:
                    sp.wait_ge(unit_lo, u - RAW + 1)
                    om, ob, ok = units[u - RAW]
                    if folds(om, ob):
                        sp.wait_ge(folded_stored[u % RAW], stored_count(ok))
                if m == "w1" and b and k == 0:
                    for ok in range(KT):
                        sp.wait_ge(folded_stored[unit_no["w1", 0, ok] % RAW], stored_count(ok))
                sp.dma_start(raw[:, u % RAW, :], unit_source(m, b, k)).then_inc(raw_in[u % RAW], 16)

        @block.gpsimd
        def _(pool):
            steps = [0]

            def own(ins):
                steps[0] += 1
                ins.then_inc(pool_step, 1)
                pool.wait_ge(pool_step, steps[0])

            own(nc.gpsimd.memset(ident[:, :], 0.0))
            own(nc.gpsimd.affine_select(out=ident[:, :], in_=ident[:, :], compare_op=ALU.not_equal, fill=1.0,
                                        base=0, pattern=[[-1, P]], channel_multiplier=1))
            nc.gpsimd.tensor_copy(ident16[:, :], ident[:, :])
            nc.gpsimd.memset(ones16[:, :], 1.0)
            nc.gpsimd.memset(minus_half, -0.5)
            for e in range(EXPERTS):
                last = nc.gpsimd.memset(expert_no[:, e:e + 1], float(e))
            own(last)
            nc.gpsimd.memset(top_w, 0.0).then_inc(consts_ready, 1)

            def inverse_deviation(n):
                _, s, t = SEQ[n]
                pool.wait_ge(input_var_ready if s == QMM else var_ready, norm_no(n) + 1)
                power = nc.gpsimd.tensor_tensor(out=rstd[:, t:t + 1], in0=var_eps[:, t:t + 1], in1=minus_half, op=ALU.pow)
                if s != QMM:
                    power.then_inc(rstd_ready, 1)
                    return
                own(power)
                if nth[QMM][n]:
                    pool.wait_ge(y1_ready, nth[QMM][n])
                own(nc.gpsimd.tensor_tensor(out=q_scale, in0=rstd[:, t:t + 1], in1=inv_s1, op=ALU.mult))
                own(nc.gpsimd.tensor_tensor(out=q_mean, in0=mv[:, 2 * t:2 * t + 1], in1=q_scale, op=ALU.mult))
                nc.gpsimd.tensor_tensor(out=q_shift, in0=z1, in1=q_mean, op=ALU.subtract).then_inc(input_rstd_ready, 1)

            def add_vector(n):
                _, s, t = SEQ[n]
                if s == QMM:
                    pool.wait_ge(x_row_added, nth[QMM][n] + 1)
                    pool.wait_ge(col_term_ready, SEQ[n][0] + 1)
                else:
                    pool.wait_ge(rows_ready, nth_float[n] + 1)
                    pool.wait_ge(bias_in, 16 * (2 * SEQ[n][0] + (1 if s == FFN0 else 2)))
                nc.gpsimd.tensor_tensor(out=x_sb[:, t, :], in0=x_sb[:, t, :], in1=(col_term if s == QMM else bias)[:, :],
                                        op=ALU.add).then_inc(x_added, 1)

            pool.wait_ge(scalars_ready, 1)
            inverse_deviation(POS[0, QMM, 0])
            inverse_deviation(POS[0, QMM, 1])
            inverse_deviation(POS[0, QMM, 2])
            for n in range(N):
                if n and SEQ[n - 1][1] in NEXT_NORM:
                    b, s, t = SEQ[n - 1]
                    inverse_deviation(POS[b, NEXT_NORM[s], t])
                if n in nth_added:
                    add_vector(n)
                if n in NORM_X:
                    b, t = NORM_X[n]
                    inverse_deviation(POS[b, QMM, t])

        @block.vector
        def _(dve):
            steps = [0]

            def own(ins):
                steps[0] += 1
                ins.then_inc(dve_step, 1)
                dve.wait_ge(dve_step, steps[0])

            def norm_stats(n):
                _, s, t = SEQ[n]
                ready = input_var_ready if s == QMM else var_ready
                st = stats.rearrange("p (h c) -> p h c", h=2)
                nc.vector.bn_stats(out=st[:, 0, :], in_=x_sb[:, t, 0:HALF])
                own(nc.vector.bn_stats(out=st[:, 1, :], in_=x_sb[:, t, HALF:D]))
                own(nc.vector.bn_aggr(out=mv[:, 2 * t:2 * t + 2], in_=st))
                nc.vector.tensor_scalar(var_eps[:, t:t + 1], mv[:, 2 * t + 1:2 * t + 2], EPS, None,
                                        ALU.add).then_inc(ready, 1)
                dve.wait_ge(ready, norm_no(n) + 1)

            def round_q(dst, v):
                own(nc.vector.tensor_scalar(v, v, MAGIC, MAGIC, ALU.add, ALU.max))
                return nc.vector.tensor_scalar(dst, v, MAGIC + QMAX, MAGIC + MID, ALU.min, ALU.subtract)

            def make_rows(n):
                b, s, t = SEQ[n]
                if s == QMM:
                    if nth[QMM][n]:
                        before = [m for m in range(n) if SEQ[m][1] == QMM][-1]
                        dve.wait_ge(tr_done, 2 * before + 2)
                        dve.wait_ge(row_term_ready, nth[QMM][n])
                    dve.wait_ge(y1_ready, nth[QMM][n] + 1)
                    round_q(q1[:, :], rows[:, :]).then_inc(q1_ready, 1)
                    return
                if n:
                    if SEQ[n - 1][1] == QMM:
                        dve.wait_ge(q1_ready, nth[QMM][n - 1] + 1)
                    else:
                        dve.wait_ge(tr_done, 2 * (n - 1) + 2)
                if s == PV:
                    nc.vector.tensor_scalar(rows[:, :], e_sb[:, t, :], e_inv[:, t:t + 1], None,
                                            ALU.mult).then_inc(rows_ready, 1)
                    return
                dve.wait_ge(rstd_ready, norm_no(n) + 1)
                nc.vector.tensor_scalar(rows[:, :], x_sb[:, t, :], mv[:, 2 * t:2 * t + 1], rstd[:, t:t + 1],
                                        ALU.subtract, ALU.mult).then_inc(rows_ready, 1)

            def split_low_half(n):
                for h in range(2):
                    ks = slice(h * KH, (h + 1) * KH)
                    dve.wait_ge(hi_done, 2 * n + h + 1)
                    nc.vector.tensor_tensor(out=rt_lo[:, n % 2, ks, :],
                                            in0=tp[:, h, :].rearrange("p (k r) -> p k r", k=KH),
                                            in1=rt_hi[:, n % 2, ks, :].bitcast(F32),
                                            op=ALU.subtract).then_inc(lo_done, 1)

            def fold_unit(u):
                m, b, k = units[u]
                dve.wait_ge(raw_in[u % RAW], 16 * (u // RAW + 1))
                dve.wait_ge(fold_done, k + 1)
                for h, ps in enumerate((low_ps, lowt_ps)):
                    part = raw[:, u % RAW, h * HALF:(h + 1) * HALF]
                    both = nc.vector.tensor_tensor(out=part, in0=ps[:, :], in1=part, op=ALU.add)
                both.then_inc(folded, 1)

            def do_unit(u):
                m, b, k = units[u]
                src = unit_raw(u)
                dve.wait_ge(unit_hi, u + 1)
                if m == "q2":
                    dve.wait_ge(rows_ready, nth_float[POS[b - 1, PV, k // 2]] + 1)
                    round_q(q2[:, k, :], src).then_inc(unit_lo, 1)
                    return
                hi, lo = unit_dest(m, k)
                if m == "lora1a":
                    dve.wait_ge(coef_in, 16)
                    nc.vector.tensor_scalar(coef, coef_raw, SCALING, None, ALU.mult).then_inc(coef_ready, 1)
                if m == "lora1b":
                    dve.wait_ge(coef_ready, 1)
                    nc.vector.scalar_tensor_tensor(out=lo, in0=src, scalar=coef, in1=hi.bitcast(F32),
                                                   op0=ALU.mult, op1=ALU.subtract).then_inc(unit_lo, 1)
                else:
                    nc.vector.tensor_tensor(out=lo, in0=src, in1=hi.bitcast(F32), op=ALU.subtract).then_inc(unit_lo, 1)
                if m == "lora0a":
                    dve.wait_ge(gate_hi, b + 1)
                    nc.vector.tensor_tensor(out=a_parts[:, :, 1, ER:], in0=gate_raw[:, :, :],
                                            in1=a_parts[:, :, 0, ER:].bitcast(F32), op=ALU.subtract).then_inc(gate_lo, 1)

            def do_first_unit(k):
                dve.wait_ge(first_hi, KT + k + 1)
                nc.vector.tensor_tensor(out=r0_lo[:, k, :], in0=first_w0[:, k, :], in1=r0_hi[:, k, :].bitcast(F32),
                                        op=ALU.subtract).then_inc(first_lo, 1)

            def column_term(b):
                if b:
                    dve.wait_ge(x_added, nth_added[POS[b - 1, QMM, TILES - 1]] + 1)
                dve.wait_ge(colsum_done, b + 1)
                nc.vector.tensor_scalar(col_term[:, 0:HALF], low_ps[:, :], col_add, col_f, ALU.add, ALU.mult)
                nc.vector.tensor_scalar(col_term[:, HALF:D], lowt_ps[:, :], col_add, col_f, ALU.add,
                                        ALU.mult).then_inc(col_term_ready, 1)

            def take_sums(n):
                b, s, t = SEQ[n]
                dve.wait_ge(acc_done, n + 1)
                a, xt = acc[:, n % 2, :], x_sb[:, t, :]
                if s == QK:
                    own(nc.vector.tensor_reduce(out=neg_max[:, 0:1], in_=a, axis=AX.X, op=ALU.max))
                    if nth[QK][n]:
                        dve.wait_ge(exp_done, nth[QK][n])
                    nc.vector.tensor_scalar(neg_max[:, 1:2], neg_max[:, 0:1], -1.0, None,
                                            ALU.mult).then_inc(max_ready, 1)
                    return
                if s != PV:
                    dve.wait_ge(x_added, nth_added[n] + 1)
                if s == QMM:
                    added = nc.vector.scalar_tensor_tensor(out=xt, in0=a, scalar=s12, in1=xt, op0=ALU.mult, op1=ALU.add)
                else:
                    added = nc.vector.tensor_tensor(out=xt, in0=a, in1=xt, op=ALU.add)
                added.then_inc(acc_free, 1)
                dve.wait_ge(acc_free, n + 1)
                if s != FFN1:
                    norm_stats(POS[b, NEXT_NORM[s], t])

            def invert_sum(n):
                t = SEQ[n][2]
                dve.wait_ge(exp_done, nth[QK][n] + 1)
                nc.vector.reciprocal(e_inv[:, t:t + 1], e_sum[:, t:t + 1]).then_inc(acc_free, 1)
                dve.wait_ge(acc_free, n + 1)

            def low_rank(n):
                s = SEQ[n][1]
                dve.wait_ge(low_done, nth[FFN0][n] + 1)
                if nth[FFN0][n]:
                    dve.wait_ge(lowt_done, nth[FFN0][n])
                own(nc.vector.tensor_copy(low[:, :], low_ps[:, LOW:2 * LOW]))
                own(nc.vector.tensor_tensor(out=low[:, :], in0=low_ps[:, 0:LOW], in1=low[:, :], op=ALU.add))
                logits = low[:, ER:]
                own(nc.vector.max(out=top, in_=logits))
                nc.vector.max_index(out=idx[:, :], in_max=top, in_values=logits)
                nc.vector.tensor_tensor(out=gap, in0=top[:, 1:2], in1=top[:, 0:1], op=ALU.subtract).then_inc(gap_ready, 1)
                dve.wait_ge(gap_ready, nth[FFN0][n] + 1)
                own(nc.vector.tensor_copy(idx_f, idx[:, 0:TOP]))
                dve.wait_ge(gap_exp_ready, nth[FFN0][n] + 1)
                own(nc.vector.tensor_scalar(gap_den, gap_exp, 1.0, None, ALU.add))
                own(nc.vector.reciprocal(top_w[:, 0:1], gap_den))
                own(nc.vector.tensor_tensor(out=top_w[:, 1:2], in0=gap_exp, in1=top_w[:, 0:1], op=ALU.mult))
                for i in range(TOP):
                    oh = nc.vector.tensor_scalar(one_hot[:, i * EXPERTS:(i + 1) * EXPERTS], expert_no,
                                                 idx_f[:, i:i + 1], top_w[:, i:i + 1], ALU.is_equal, ALU.mult)
                own(oh)
                own(nc.vector.tensor_tensor(out=expert_w, in0=one_hot[:, 0:EXPERTS], in1=one_hot[:, EXPERTS:], op=ALU.add))
                nc.vector.scalar_tensor_tensor(
                    out=low_s[:, :].rearrange("p (e r) -> p e r", e=EXPERTS),
                    in0=low[:, 0:ER].rearrange("p (e r) -> p e r", e=EXPERTS), scalar=SCALING,
                    in1=expert_w.unsqueeze(2).to_broadcast([P, EXPERTS, RANK]),
                    op0=ALU.mult, op1=ALU.mult).then_inc(low_ready, 1)

            def split_low_rank(n):
                dve.wait_ge(lowt_hi_done, nth[FFN0][n] + 1)
                nc.vector.tensor_tensor(out=lowt_lo[:, :], in0=lowt_ps[:, 0:P], in1=lowt_hi[:, :].bitcast(F32),
                                        op=ALU.subtract).then_inc(lowt_lo_done, 1)

            dve.wait_ge(scalars_in, 16)
            nc.vector.reciprocal(inv_s1, s1)
            nc.vector.reciprocal(inv_s2, s2)
            nc.vector.tensor_scalar(d2, z2, -1.0, MID, ALU.mult, ALU.add)
            nc.vector.tensor_scalar(col_f, z1, -1.0, MID, ALU.mult, ALU.add)
            own(nc.vector.tensor_tensor(out=s12, in0=s1, in1=s2, op=ALU.mult))
            nc.vector.tensor_tensor(out=row_f, in0=s12, in1=d2, op=ALU.mult)
            nc.vector.tensor_tensor(out=col_f, in0=s12, in1=col_f, op=ALU.mult)
            nc.vector.tensor_scalar(col_add, d2, float(D), None, ALU.mult).then_inc(scalars_ready, 1)
            dve.wait_ge(scalars_ready, 1)
            dve.wait_ge(x_in[0], 16)
            norm_stats(POS[0, QMM, 0])
            for k in range(KT):
                if k == 2:
                    make_rows(0)
                if k == 4:
                    dve.wait_ge(x_in[1], 16)
                    norm_stats(POS[0, QMM, 1])
                if k == KT - 1:
                    make_rows(1)
                dve.wait_ge(first_hi, k + 1)
                round_q(q2[:, k, :], first_ctx[:, k, :]).then_inc(first_lo, 1)
            dve.wait_ge(x_in[2], 16)
            norm_stats(POS[0, QMM, 2])
            dve.wait_ge(consts_ready, 1)
            for n in range(N):
                b, s, t = SEQ[n]
                nxt = n + 1
                todo = [(do_first_unit, k) for k in first_units.get(n, [])]
                for m, ub, k in window_units[n]:
                    if folds(m, ub):
                        todo.append((fold_unit, unit_no[m, ub, k]))
                    todo.append((do_unit, unit_no[m, ub, k]))

                def some(keep):
                    while len(todo) > keep:
                        do, u = todo.pop(0)
                        do(u)

                if SEQ[n - 1] == (0, QMM, 0):
                    column_term(0)
                if n:
                    take_sums(n - 1)
                if b and (s, t) == (QMM, 0):
                    column_term(b)
                if MAKE_FIRST[n]:
                    make_rows(MAKE_FIRST[n])
                if s == FFN0:
                    some(max(len(todo) - 1, 0))
                    low_rank(n)
                if n and SEQ[n - 1][1] == QK:
                    invert_sum(n - 1)
                if s == PV:
                    some(max(len(todo) - 1, 0) if len(todo) < 3 else len(todo) - 1)
                elif s != QMM:
                    some(0 if n in first_units or len(todo) == 1 else len(todo) // 2)
                if nxt < N and SEQ[nxt][1] != QMM:
                    split_low_half(nxt)
                if s == FFN0:
                    split_low_rank(n)
                if MAKE_LAST[n] and is_quant(n):
                    make_rows(MAKE_LAST[n])
                some(0)
                if MAKE_LAST[n] and not is_quant(n):
                    make_rows(MAKE_LAST[n])
                if n in NORM_X:
                    nb, nt = NORM_X[n]
                    dve.wait_ge(x_in[nt], 16 * (nb + 1))
                    norm_stats(POS[nb, QMM, nt])
            take_sums(N - 1)

        @block.scalar
        def _(act):
            def scale_rows(n):
                t = SEQ[n][2]
                act.wait_ge(input_rstd_ready, nth[QMM][n] + 1)
                if n:
                    if SEQ[n - 1][1] == QMM:
                        act.wait_ge(q1_ready, nth[QMM][n - 1] + 1)
                    else:
                        act.wait_ge(tr_done, 2 * (n - 1) + 2)
                nc.scalar.activation(rows[:, :], x_sb[:, t, :], ACT.Identity, bias=q_shift,
                                     scale=q_scale).then_inc(y1_ready, 1)

            def add_row_term(n):
                t = SEQ[n][2]
                act.wait_ge(tr_done, 2 * n + 2)
                nc.scalar.activation(q1[:, :], q1[:, :], ACT.Copy, scale=row_f,
                                     accum_out=row_term[:, t:t + 1]).then_inc(row_term_ready, 1)
                act.wait_ge(row_term_ready, nth[QMM][n] + 1)
                nc.scalar.activation(x_sb[:, t, :], x_sb[:, t, :], ACT.Identity,
                                     bias=row_term[:, t:t + 1]).then_inc(x_row_added, 1)

            def split_high_half(n):
                s = SEQ[n][1]
                for h in range(2):
                    ks = slice(h * KH, (h + 1) * KH)
                    act.wait_ge(tr_done, 2 * n + h + 1)
                    if s == QMM:
                        src = tp[:, h, 0:HALF // 2].bitcast(BF16).rearrange("p (k r) -> p k r", k=KH)
                        dst = q1_t[n % 2][:, ks, :]
                    else:
                        src = tp[:, h, :].rearrange("p (k r) -> p k r", k=KH)
                        dst = rt_hi[:, n % 2, ks, :]
                    nc.scalar.activation(dst, src, ACT.Copy).then_inc(hi_done, 1)

            def do_unit(u):
                m, b, k = units[u]
                src = unit_raw(u)
                act.wait_ge(raw_in[u % RAW], 16 * (u // RAW + 1))
                if folds(m, b):
                    act.wait_ge(folded, k + 1)
                    act.dma_start(w1_folded[k * P:(k + 1) * P, :], src).then_inc(folded_stored[u % RAW], 16)
                reader = last_reader(m, b)
                if reader is not None:
                    act.wait_ge(acc_done, reader + 1)
                if m == "kt" and b == 0:
                    act.wait_ge(first_lo, 2 * KT)
                if m == "q2":
                    nc.scalar.activation(src, src, ACT.Identity, bias=z2, scale=inv_s2).then_inc(unit_hi, 1)
                    return
                hi, _ = unit_dest(m, k)
                if m == "lora1b":
                    act.wait_ge(coef_ready, 1)
                scale = coef if m == "lora1b" else 1.0
                nc.scalar.activation(hi, src, ACT.Copy, scale=scale).then_inc(unit_hi, 1)
                if m == "lora0a":
                    act.wait_ge(gate_in, 16)
                    nc.scalar.activation(a_parts[:, :, 0, ER:], gate_raw[:, :, :], ACT.Copy).then_inc(gate_hi, 1)

            def do_first_unit(k):
                act.wait_ge(first_w0_in[k], 16)
                nc.scalar.activation(r0_hi[:, k, :], first_w0[:, k, :], ACT.Copy).then_inc(first_hi, 1)

            def exponentials(n):
                t = SEQ[n][2]
                act.wait_ge(max_ready, nth[QK][n] + 1)
                nc.scalar.activation(e_sb[:, t, :], acc[:, n % 2, :], ACT.Exp, bias=neg_max[:, 1:2],
                                     accum_out=e_sum[:, t:t + 1]).then_inc(exp_done, 1)

            def load_bias(b, s):
                if (b, s) != (0, FFN0):
                    last = (b - 1, FFN1, TILES - 1) if s == FFN0 else (b, FFN0, TILES - 1)
                    act.wait_ge(x_added, nth_added[POS[last]] + 1)
                act.dma_start(bias[:, :], (b0 if s == FFN0 else b1).partition_broadcast(P)).then_inc(bias_in, 16)

            def store(n):
                b, _, t = SEQ[n]
                act.wait_ge(acc_free, n + 1)
                act.dma_start(out[b, t * P:(t + 1) * P, :], x_sb[:, t, :]).then_inc(out_done[t], 16)

            act.wait_ge(consts_ready, 1)
            nc.scalar.activation(gap_exp, minus_half, ACT.Exp).then_inc(table_loaded, 1)
            act.wait_ge(scalars_ready, 1)
            for k in range(KT):
                if k == 1:
                    scale_rows(0)
                if k == 5:
                    split_high_half(0)
                    add_row_term(0)
                if k == 6:
                    scale_rows(1)
                act.wait_ge(first_ctx_in[k], 16)
                nc.scalar.activation(first_ctx[:, k, :], first_ctx[:, k, :], ACT.Identity, bias=z2,
                                     scale=inv_s2).then_inc(first_hi, 1)
            for n in range(N):
                b, s, t = SEQ[n]
                nxt = n + 1
                todo = [(do_unit, unit_no[u]) for u in window_units[n]] + [(do_first_unit, k) for k in first_units.get(n, [])]

                def some(keep):
                    while len(todo) > keep:
                        do, u = todo.pop(0)
                        do(u)

                if n and SEQ[n - 1][1] == QK:
                    exponentials(n - 1)
                if MAKE_FIRST[n] and is_quant(MAKE_FIRST[n]):
                    scale_rows(MAKE_FIRST[n])
                if n and SEQ[n - 1][1] == FFN1:
                    store(n - 1)
                if s == FFN0:
                    some(max(len(todo) - 1, 0))
                    act.wait_ge(gap_ready, nth[FFN0][n] + 1)
                    nc.scalar.activation(gap_exp, gap, ACT.Exp).then_inc(gap_exp_ready, 1)
                if s == PV:
                    some(max(len(todo) - 1, 0) if folds("w1", b) else len(todo) // 2)
                elif s != QMM:
                    some(0 if n in first_units or len(todo) == 1 else len(todo) // 2)
                if nxt < N:
                    split_high_half(nxt)
                    if is_quant(nxt):
                        add_row_term(nxt)
                if n in LOAD_BIAS:
                    load_bias(*LOAD_BIAS[n])
                if n in LOAD_X:
                    lb, lt = LOAD_X[n]
                    act.wait_ge(out_done[lt], 16 * lb)
                    act.dma_start(x_sb[:, lt, :], x[lb, lt * P:(lt + 1) * P, :]).then_inc(x_in[lt], 16)
                if s == FFN0:
                    act.wait_ge(lowt_done, nth[FFN0][n] + 1)
                    nc.scalar.activation(lowt_hi[:, :], lowt_ps[:, 0:P], ACT.Copy).then_inc(lowt_hi_done, 1)
                if MAKE_LAST[n] and is_quant(MAKE_LAST[n]):
                    scale_rows(MAKE_LAST[n])
                some(0)
            store(N - 1)
            for t in range(TILES):
                act.wait_ge(out_done[t], 16 * BATCHES)

        @block.tensor
        def _(pe):
            def transposes(n):
                s = SEQ[n][1]
                if s == QMM:
                    pe.wait_ge(q1_ready, nth[QMM][n] + 1)
                else:
                    pe.wait_ge(rows_ready, nth_float[n] + 1)
                for h in range(2):
                    for i in range(KH):
                        k = h * KH + i
                        if s == QMM:
                            dst = tp[:, h, 0:HALF // 2].bitcast(BF16)[:, i * P:(i + 1) * P]
                            last = nc.tensor.transpose(dst, q1[:, k * P:(k + 1) * P], ident16[:, :])
                        else:
                            last = nc.tensor.transpose(tp[:, h, i * P:(i + 1) * P],
                                                       rows[:, k * P:(k + 1) * P], ident[:, :])
                    last.then_inc(tr_done, 1)

            def matrix_ready(s, b, k):
                if s == FFN0 and b == 0:
                    pe.wait_ge(first_lo, KT + k + 1)
                elif s == QMM and b == 0:
                    pe.wait_ge(first_lo, k + 1)
                else:
                    m = {QMM: "q2", FFN0: "w0", QK: "kt", PV: "v", FFN1: "w1"}[s]
                    pe.wait_ge(unit_lo, unit_no[m, b, k] + 1)

            def rows_split(n, h):
                if SEQ[n][1] == QMM:
                    pe.wait_ge(hi_done, 2 * n + h + 1)
                else:
                    pe.wait_ge(lo_done, 2 * nth_float[n] + h + 1)

            def column_sums(b, k):
                for h, dst in enumerate((low_ps, lowt_ps)):
                    last = nc.tensor.matmul(dst[:, :], ones16[:, :], q2[:, k, h * HALF:(h + 1) * HALF],
                                            start=(k == 0), stop=(k == KT - 1))
                if k == KT - 1:
                    last.then_inc(colsum_done, 1)

            PASSES = ((0, 0), (0, 1), (1, 0))

            def fold(k):
                if k == 0:
                    pe.wait_ge(unit_lo, unit_no["lora1b", 0, 0] + 1)
                else:
                    pe.wait_ge(folded, k)
                for h, dst in enumerate((low_ps, lowt_ps)):
                    for i, (l, r) in enumerate(PASSES):
                        last = nc.tensor.matmul(dst[:, :], a_parts[:, k, l, 0:P], (bb_hi, bb_lo)[r][:, h * HALF:(h + 1) * HALF],
                                                start=(i == 0), stop=(i == 2))
                last.then_inc(fold_done, 1)

            pe.wait_ge(consts_ready, 1)
            transposes(0)
            for n in range(N):
                b, s, t = SEQ[n]
                p = n % 2
                if b and (s, t) == (QMM, 0):
                    for k in range(KT):
                        matrix_ready(QMM, b, k)
                        column_sums(b, k)
                left = (rt_hi, rt_lo)
                right = {FFN0: (r0_hi, r0_lo), QK: (r1_hi, r1_lo), PV: (r0_hi, r0_lo), FFN1: (r1_hi, r1_lo)}.get(s)
                to_fold = [k for m, ub, k in window_units[n] if folds(m, ub)]
                rows_split(n, 0)
                if n >= 2:
                    pe.wait_ge(acc_free, n - 1)
                for k in range(KT):
                    if k == TRANSPOSE_AT[n] and n + 1 < N:
                        rows_split(n, 1)
                        transposes(n + 1)
                    if k == KH:
                        rows_split(n, 1)
                    if t == 0:
                        matrix_ready(s, b, k)
                    if s == QMM:
                        if n == 0:
                            column_sums(b, k)
                        for h in range(2):
                            last = nc.tensor.matmul(acc[:, p, h * HALF:(h + 1) * HALF], q1_t[p][:, k, :],
                                                    q2[:, k, h * HALF:(h + 1) * HALF], start=(k == 0), stop=(k == KT - 1))
                        continue
                    if to_fold and k % 3 == 0:
                        fold(to_fold.pop(0))
                    end = k == KT - 1 and s != FFN0
                    for i, (l, r) in enumerate(PASSES):
                        for h in range(2):
                            last = nc.tensor.matmul(acc[:, p, h * HALF:(h + 1) * HALF], left[l][:, p, k, :],
                                                    right[r][:, k, h * HALF:(h + 1) * HALF],
                                                    start=(k == 0 and i == 0), stop=(end and i == 2))
                    if s == FFN0 and k == 1:
                        rows_split(n, 1)
                        if t == 0:
                            pe.wait_ge(unit_lo, unit_no["lora0a", b, 0] + 1)
                            pe.wait_ge(gate_lo, b + 1)
                            pe.wait_ge(col_term_ready, b + 1)
                        for kk in range(KT):
                            nc.tensor.matmul(low_ps[:, 0:2 * LOW], rt_hi[:, p, kk, :],
                                             a_parts[:, kk, :, :].rearrange("p c e -> p (c e)"),
                                             start=(kk == 0), stop=False)
                            low_last = nc.tensor.matmul(low_ps[:, 0:LOW], rt_lo[:, p, kk, :], a_parts[:, kk, 0, :],
                                                        start=False, stop=(kk == KT - 1))
                        low_last.then_inc(low_done, 1)
                    if s == FFN0 and k == KT - 2:
                        pe.wait_ge(low_ready, nth[FFN0][n] + 1)
                        nc.tensor.transpose(lowt_ps[:, 0:P], low_s[:, :], ident[:, :]).then_inc(lowt_done, 1)
                if s == FFN0:
                    if t == 0:
                        pe.wait_ge(unit_lo, unit_no["lora0b", b, 0] + 1)
                    pe.wait_ge(lowt_lo_done, nth[FFN0][n] + 1)
                    lt = (lowt_hi, lowt_lo)
                    for i, (l, r) in enumerate(PASSES):
                        for h in range(2):
                            last = nc.tensor.matmul(acc[:, p, h * HALF:(h + 1) * HALF], lt[l][:, :],
                                                    (bb_hi, bb_lo)[r][:, h * HALF:(h + 1) * HALF], start=False, stop=(i == 2))
                last.then_inc(acc_done, 1)


def kernel(x, ctx_4096, L0_xattn_x1_scale, L0_xattn_x1_zp, L0_xattn_x2_scale, L0_xattn_x2_zp, L0_ffn_gate_w,
           L0_ffn_base_w, L0_ffn_base_b, L0_ffn_lora_A, L0_ffn_lora_B, L1_ffn_lora_A, L1_ffn_lora_B, L1_ffn_W,
           L1_ffn_bias, L1_ffn_lora_weights):
    import numpy as np
    import concourse.bacc as bacc
    from concourse.bass_utils import run_bass_kernel_spmd

    P = 128
    c = np.ascontiguousarray

    def k_tiles(m):
        m = np.asarray(m)
        return c(m.reshape(-1, P, m.shape[1]).transpose(1, 0, 2).reshape(P, -1))

    lora_a_t = lambda a: k_tiles(np.asarray(a).reshape(-1, a.shape[2]).T)
    lora_b_t = lambda a: c(np.asarray(a).transpose(0, 2, 1).reshape(-1, a.shape[1]))
    rank = L1_ffn_lora_A.shape[1]
    arrays = {
        "x": c(x), "ctx": c(ctx_4096), "ctx_t": c(np.asarray(ctx_4096).transpose(0, 2, 1)),
        "q_scalars": np.concatenate([L0_xattn_x1_scale, L0_xattn_x1_zp, L0_xattn_x2_scale, L0_xattn_x2_zp]),
        "gate_t": k_tiles(np.asarray(L0_ffn_gate_w).T), "w0_t": c(np.asarray(L0_ffn_base_w).T), "b0": c(L0_ffn_base_b),
        "a0_t": lora_a_t(L0_ffn_lora_A), "bb0_t": lora_b_t(L0_ffn_lora_B),
        "a1": c(np.asarray(L1_ffn_lora_A).reshape(-1, L1_ffn_lora_A.shape[2])), "bb1_t": lora_b_t(L1_ffn_lora_B),
        "w1_t": c(np.asarray(L1_ffn_W).T), "b1": c(L1_ffn_bias),
        "lora_w": c(np.repeat(np.asarray(L1_ffn_lora_weights), rank).reshape(-1, 1)),
    }
    nc = bacc.Bacc("TRN2", target_bir_lowering=False, num_devices=1, dynamic_dma_scratch_size=1024)
    dram = {n: nc.dram_tensor(n, a.shape, mybir.dt.from_np(a.dtype), kind="ExternalInput").ap() for n, a in arrays.items()}
    out = nc.dram_tensor("out", arrays["x"].shape, mybir.dt.float32, kind="ExternalOutput").ap()
    g = dram["gate_t"].rearrange("p (k e) -> p k e", e=L0_ffn_gate_w.shape[0])
    two_layer_kernel(nc, dram["x"], dram["ctx"], dram["ctx_t"], dram["q_scalars"], g,
                     dram["w0_t"], dram["b0"], dram["a0_t"], dram["bb0_t"], dram["a1"], dram["bb1_t"], dram["w1_t"],
                     dram["b1"], dram["lora_w"], out)
    got = run_bass_kernel_spmd(nc, [arrays], core_ids=[0])
    return got.results[0]["out"]
```

```python
from concourse import mybir
from contextlib import ExitStack

F32 = mybir.dt.float32
F32R = mybir.dt.float32r
BF16 = mybir.dt.bfloat16
U32 = mybir.dt.uint32
ALU = mybir.AluOpType
ACT = mybir.ActivationFunctionType
AX = mybir.AxisListType


def two_layer_kernel(nc, x, ctx, ctx_t, q_scalars, gate_t, w0_t, b0, a0_t, bb0_t, a1, bb1_t, w1_t, b1, lora_w, out):
    P = nc.NUM_PARTITIONS
    BATCHES, ROWS, D = x.shape
    KT = D // P
    TILES = ROWS // P
    HALF = D // 2
    KH = KT // 2
    EXPERTS, RANK = 8, 16
    ER = EXPERTS * RANK
    LOW = ER + EXPERTS
    TOP = 2
    SCALING = 2.0
    EPS = 1e-5
    QMAX = 255.0
    MID = 128.0
    MAGIC = 12582912.0
    QMM, FFN0, QK, PV, FFN1 = STAGES = range(5)
    JOBS = len(STAGES) * TILES
    RAW = 3

    SEQ = []
    for b in range(BATCHES):
        first = [(b, QMM, 0), (b, QMM, 1), (b, QMM, 2), (b, FFN0, 0), (b, QMM, 3), (b, FFN0, 1), (b, FFN0, 2), (b, FFN0, 3)]
        if b:
            first = [(b, QMM, 0), SEQ.pop(), (b, QMM, 1), (b, FFN0, 0), (b, QMM, 2), (b, FFN0, 1), (b, QMM, 3),
                     (b, FFN0, 2), (b, FFN0, 3)]
        SEQ += first + [(b, s, t) for s in (QK, PV, FFN1) for t in range(TILES)]
    N = len(SEQ)
    POS = {j: n for n, j in enumerate(SEQ)}

    def rank(*stages):
        of = [n for n in range(N) if SEQ[n][1] in stages]
        return {n: i for i, n in enumerate(of)}

    nth = {s: rank(s) for s in STAGES}
    nth_float = rank(FFN0, QK, PV, FFN1)
    nth_added = rank(QMM, FFN0, FFN1)
    nth_normed = rank(QMM, FFN0, PV)
    NEXT_NORM = {QMM: FFN0, FFN0: QK, PV: FFN1}
    PREV_SUM = {v: k for k, v in NEXT_NORM.items()}

    def norm_no(n):
        b, s, t = SEQ[n]
        return nth[QMM][n] if s == QMM else nth_normed[POS[b, PREV_SUM[s], t]]

    LOAD_X = {POS[j]: (b, t) for b in range(1, BATCHES) for t, j in enumerate(
        [(b - 1, FFN1, 1), (b - 1, FFN1, 2), (b - 1, FFN1, 3), (b, FFN0, 0)])}
    NORM_X = {POS[j]: (b, t) for b in range(1, BATCHES) for t, j in enumerate(
        [(b - 1, FFN1, 1), (b, QMM, 0), (b, QMM, 1), (b, QMM, 2)])}
    NORM_X |= {POS[0, QMM, 2]: (0, 3)}

    is_quant = lambda n: 0 <= n < N and SEQ[n][1] == QMM
    MAKE_FIRST = [n + 1 if n + 1 < N and not is_quant(n) else None for n in range(N)]
    MAKE_LAST = [n + 2 if n + 2 < N and is_quant(n + 1) else None for n in range(N)]
    TRANSPOSE_AT = [KT if n in (1, 2, 3) else KT - 2 if is_quant(n + 1) else 0 if is_quant(n) else KH for n in range(N)]

    SUM_Q2 = {POS[b - 1, FFN1, t]: [(b, k) for k in ks] for b in range(1, BATCHES)
              for t, ks in enumerate([(1, 2), (3, 4), (5, 6, 7)])}

    LOW_AT = [3 if n == POS[0, FFN0, 0] else 1 for n in range(N)]
    LOWT_AT = [KT - 2 if is_quant(n + 1) else KT - 3 for n in range(N)]

    LOAD_BIAS = {POS[j]: (b, s) for b in range(BATCHES) for s, j in ((FFN0, (b, QMM, 1)), (FFN1, (b, QK, 0)))}

    def lot(m, b, first, count):
        return [(m, b, k) for k in range(first, first + count)]

    window_units = {n: [] for n in range(N)}
    first_w0_hi = {POS[0, QMM, 0]: [1], POS[0, QMM, 1]: [2, 3], POS[0, QMM, 2]: [4, 5, 6, 7]}
    first_w0_dve = {POS[0, QMM, 2]: [3, 4]}
    first_w0_pool = {POS[0, QMM, 1]: [1, 2], POS[0, QMM, 2]: [5, 6], POS[0, FFN0, 0]: [7]}
    DVE_W0, POOL_W0 = sum(first_w0_dve.values(), []), sum(first_w0_pool.values(), [0])
    for b in range(BATCHES):
        plan = [((b - 1, FFN1, 1) if b else (b, QMM, 2), [("lora0a", b, 0)]),
                ((b - 1, FFN1, 2) if b else (b, QMM, 2), [("lora0b", b, 0)]),
                ((b, FFN0, 1), lot("kt", b, 0, 3)), ((b, FFN0, 2), lot("kt", b, 3, 3)), ((b, FFN0, 3), lot("kt", b, 6, 2)),
                ((b, QK, 0), lot("v", b, 0, 3)), ((b, QK, 1), lot("v", b, 3, 3)), ((b, QK, 2), lot("v", b, 6, 2)),
                ((b, QK, 3), [("lora1a", b, 0), ("lora1b", b, 0)] if b == 0 else []),
                *[((b, PV, t), lot("w1", b, 2 * t, 2)) for t in range(TILES)]]
        if b + 1 < BATCHES:
            plan += [((b, FFN1, 0), lot("q2", b + 1, 0, 5)),
                     ((b, FFN1, 1), lot("q2", b + 1, 5, 3)),
                     ((b, FFN1, 2), lot("w0", b + 1, 0, 1)), ((b + 1, QMM, 0), lot("w0", b + 1, 1, 3)),
                     ((b, FFN1, 3), lot("w0", b + 1, 4, 2)), ((b + 1, FFN0, 0), lot("w0", b + 1, 6, 2))]
        for j, lots in plan:
            window_units[POS[j]] += lots
    units = [u for n in range(N) for u in window_units[n]]
    unit_no = {u: i for i, u in enumerate(units)}

    es = ExitStack()
    with es:
        at = [(nc.sbuf_base + 31) // 32 * 32]
        size = {F32: 4, F32R: 4, BF16: 2, U32: 4}

        def place(name, shape, dt, over=None):
            if over is None:
                over = at[0]
                n = size[dt]
                for d in shape[1:]:
                    n *= d
                at[0] += (n + 31) // 32 * 32
            return nc.alloc_sbuf_tensor_at(name, shape, dt, offset=over), over

        x_sb, _ = place("x_sb", [P, TILES, D], F32)
        r0_hi, _ = place("r0_hi", [P, KT, D], F32R)
        r0_lo, _ = place("r0_lo", [P, KT, D], F32R)
        r1_hi, r1_hi_at = place("r1_hi", [P, KT, D], F32R)
        r1_lo, r1_lo_at = place("r1_lo", [P, KT, D], F32R)
        first_ctx, _ = place("first_ctx", [P, KT, D], F32, over=r1_hi_at)
        first_w0, _ = place("first_w0", [P, KT, D], F32, over=r1_lo_at)
        rt_hi, _ = place("rt_hi", [P, 2, KT, P], F32R)
        rt_lo, rt_lo_at = place("rt_lo", [P, 2, KT, P], F32R)
        q1_t = [place(f"q1_t{i}", [P, KT, P], BF16, over=rt_lo_at + i * KT * P * 4)[0] for i in range(2)]
        e_sb, e_at = place("e_sb", [P, TILES, D], F32)
        q2, _ = place("q2", [P, KT, D], BF16, over=e_at)
        rows, _ = place("rows", [P, D], F32)
        q1, _ = place("q1", [P, D], BF16)
        lowt_hi, _ = place("lowt_hi", [P, P], F32R)
        lowt_lo, _ = place("lowt_lo", [P, P], F32R)
        low_s, _ = place("low_s", [P, ER], F32)
        raw, _ = place("raw", [P, RAW, D], F32)
        a_parts, _ = place("a_parts", [P, KT, 2, LOW], F32R)
        bb_hi, _ = place("bb_hi", [P, D], F32R)
        bb_lo, _ = place("bb_lo", [P, D], F32R)
        col_term, col_term_at = place("col_term", [P, D], F32)
        col_sum, _ = place("col_sum", [P, D], F32R, over=col_term_at)
        bias, _ = place("bias", [P, D], F32)
        ident, _ = place("ident", [P, P], F32)
        ident16, _ = place("ident16", [P, P], BF16)
        ones16, _ = place("ones16", [P, P], BF16)
        gate_raw, _ = place("gate_raw", [P, KT, EXPERTS], F32)
        low, _ = place("low", [P, LOW], F32)
        small, _ = place("small", [P, 112], F32)
        idx, _ = place("idx", [P, 8], U32)
        free = [0]

        def cols(n=1):
            free[0] += n
            assert free[0] <= 112
            return small[:, free[0] - n:free[0]]

        scalars = cols(4)
        s1, z1, s2, z2 = (scalars[:, i:i + 1] for i in range(4))
        inv_s1, inv_s2, s12 = cols(), cols(), cols()
        row_f, col_f, col_add, d2 = cols(), cols(), cols(), cols()
        stats, mv = cols(12), cols(2 * TILES)
        var_eps, rstd = cols(TILES), cols(TILES)
        minus_half, coef, coef_raw = cols(), cols(), cols()
        q_scale, q_shift, q_mean, row_term = cols(), cols(), cols(), cols(TILES)
        neg_max, e_sum, e_inv = cols(2), cols(TILES), cols(TILES)
        top, gap, gap_exp, gap_den, top_w, idx_f = cols(8), cols(), cols(), cols(), cols(TOP), cols(TOP)
        expert_no, one_hot, expert_w = cols(EXPERTS), cols(TOP * EXPERTS), cols(EXPERTS)

        acc = es.enter_context(nc.psum_tensor("acc", [P, 2, D], F32))
        tp = es.enter_context(nc.psum_tensor("tp", [P, 2, HALF], F32))
        low_ps = es.enter_context(nc.psum_tensor("low_ps", [P, HALF], F32))
        lowt_ps = es.enter_context(nc.psum_tensor("lowt_ps", [P, HALF], F32))

        sem = lambda name: es.enter_context(nc.semaphore(name))
        scalars_in = sem("scalars_in")
        x_in = [sem(f"x_in{t}") for t in range(TILES)]
        first_ctx_in = [sem(f"first_ctx_in{k}") for k in range(KT)]
        first_w0_in = [sem(f"first_w0_in{k}") for k in range(KT)]
        raw_in = [sem(f"raw_in{i}") for i in range(RAW)]
        coef_in = sem("coef_in")
        folded_stored = [sem(f"folded_stored{i}") for i in range(RAW)]
        gate_in = sem("gate_in")
        bias_in = sem("bias_in")
        out_done = [sem(f"out_done{t}") for t in range(TILES)]
        consts_ready = sem("consts_ready")
        pool_step = sem("pool_step")
        input_rstd_ready = sem("input_rstd_ready")
        col_sum_ready = sem("col_sum_ready")
        rstd_ready = sem("rstd_ready")
        x_added = sem("x_added")
        first_w0_lo_pool = sem("first_w0_lo_pool")
        dve_step = sem("dve_step")
        scalars_ready = sem("scalars_ready")
        coef_ready = sem("coef_ready")
        input_var_ready = sem("input_var_ready")
        var_ready = sem("var_ready")
        rows_ready = sem("rows_ready")
        q1_ready = sem("q1_ready")
        lo_done = sem("lo_done")
        first_q2 = sem("first_q2")
        first_w0_lo = sem("first_w0_lo")
        unit_lo = sem("unit_lo")
        folded = sem("folded")
        gate_lo = sem("gate_lo")
        acc_free = sem("acc_free")
        col_term_ready = sem("col_term_ready")
        max_ready = sem("max_ready")
        gap_ready = sem("gap_ready")
        low_ready = sem("low_ready")
        lowt_lo_done = sem("lowt_lo_done")
        table_loaded = sem("table_loaded")
        first_hi = sem("first_hi")
        unit_hi = sem("unit_hi")
        gate_hi = sem("gate_hi")
        y1_ready = sem("y1_ready")
        row_term_ready = sem("row_term_ready")
        x_row_added = sem("x_row_added")
        hi_done = sem("hi_done")
        exp_done = sem("exp_done")
        gap_exp_ready = sem("gap_exp_ready")
        lowt_hi_done = sem("lowt_hi_done")
        tr_done = sem("tr_done")
        acc_done = sem("acc_done")
        low_done = sem("low_done")
        lowt_done = sem("lowt_done")
        colsum_done = sem("colsum_done")
        fold_done = sem("fold_done")

        dest = {"kt": (r1_hi, r1_lo), "v": (r0_hi, r0_lo), "w1": (r1_hi, r1_lo), "w0": (r0_hi, r0_lo)}

        def unit_dest(m, k):
            if m in dest:
                return dest[m][0][:, k, :], dest[m][1][:, k, :]
            if m in ("lora0a", "lora1a"):
                return a_parts[:, :, 0, 0:ER], a_parts[:, :, 1, 0:ER]
            return bb_hi[:, :], bb_lo[:, :]

        def unit_raw(u):
            m, slot = units[u][0], raw[:, u % RAW, :]
            if m in ("lora0a", "lora1a"):
                return slot.rearrange("p (k e) -> p k e", k=KT)
            return slot

        w1_folded = nc.dram_tensor("w1_folded", [D, D], F32).ap()

        def folds(m, b):
            return m == "w1" and b == 0

        def stored_count(k):
            slot = [unit_no["w1", 0, i] % RAW for i in range(k + 1)]
            return 16 * slot.count(slot[k])

        def unit_source(m, b, k):
            r = slice(k * P, (k + 1) * P)
            if m == "w1" and b:
                return w1_folded[r, :]
            return {"kt": ctx_t[b, r, :], "v": ctx[b, r, :], "q2": ctx[b, r, :], "w1": w1_t[r, :], "w0": w0_t[r, :],
                    "lora0a": a0_t, "lora0b": bb0_t, "lora1a": a1, "lora1b": bb1_t}[m]

        def last_reader(m, b):
            last = TILES - 1
            if m == "kt":
                return POS[b - 1, FFN1, last] if b else None
            if m in ("lora0a", "lora0b"):
                return POS[b - 1, PV, last] if b else None
            if m in ("v", "lora1a", "lora1b"):
                return POS[b, FFN0, last]
            if m == "w1":
                return POS[b, QK, last]
            return POS[b - 1, PV, last] if m == "w0" else None

        block = es.enter_context(nc.Block())

        @block.sync
        def _(sp):
            def load_x(t):
                sp.dma_start(x_sb[:, t, :], x[0, t * P:(t + 1) * P, :]).then_inc(x_in[t], 16)

            sp.dma_start(scalars, q_scalars.partition_broadcast(P)).then_inc(scalars_in, 16)
            load_x(0)
            for k in range(KT):
                sp.dma_start(first_ctx[:, k, :], ctx[0, k * P:(k + 1) * P, :]).then_inc(first_ctx_in[k], 16)
                if k == 2:
                    load_x(1)
            load_x(2)
            for k in range(KH):
                sp.dma_start(first_w0[:, k, :], w0_t[k * P:(k + 1) * P, :]).then_inc(first_w0_in[k], 16)
            sp.dma_start(coef_raw, lora_w).then_inc(coef_in, 16)
            sp.dma_start(gate_raw[:, :, :], gate_t).then_inc(gate_in, 16)
            for u in range(2):
                m, b, k = units[u]
                sp.dma_start(raw[:, u % RAW, :], unit_source(m, b, k)).then_inc(raw_in[u % RAW], 16)
            load_x(3)
            for k in range(KH, KT):
                sp.dma_start(first_w0[:, k, :], w0_t[k * P:(k + 1) * P, :]).then_inc(first_w0_in[k], 16)
            for u, (m, b, k) in enumerate(units[2:], 2):
                if u >= RAW:
                    sp.wait_ge(unit_lo, u - RAW + 1)
                    om, ob, ok = units[u - RAW]
                    if folds(om, ob):
                        sp.wait_ge(folded_stored[u % RAW], stored_count(ok))
                if m == "w1" and b and k == 0:
                    for ok in range(KT):
                        sp.wait_ge(folded_stored[unit_no["w1", 0, ok] % RAW], stored_count(ok))
                sp.dma_start(raw[:, u % RAW, :], unit_source(m, b, k)).then_inc(raw_in[u % RAW], 16)

        @block.gpsimd
        def _(pool):
            steps = [0]

            def own(ins):
                steps[0] += 1
                ins.then_inc(pool_step, 1)
                pool.wait_ge(pool_step, steps[0])

            own(nc.gpsimd.memset(ident[:, :], 0.0))
            own(nc.gpsimd.affine_select(out=ident[:, :], in_=ident[:, :], compare_op=ALU.not_equal, fill=1.0,
                                        base=0, pattern=[[-1, P]], channel_multiplier=1))
            nc.gpsimd.tensor_copy(ident16[:, :], ident[:, :])
            nc.gpsimd.memset(ones16[:, :], 1.0)
            nc.gpsimd.memset(minus_half, -0.5)
            for e in range(EXPERTS):
                last = nc.gpsimd.memset(expert_no[:, e:e + 1], float(e))
            own(last)
            nc.gpsimd.memset(top_w, 0.0).then_inc(consts_ready, 1)

            def inverse_deviation(n):
                _, s, t = SEQ[n]
                pool.wait_ge(input_var_ready if s == QMM else var_ready, norm_no(n) + 1)
                power = nc.gpsimd.tensor_tensor(out=rstd[:, t:t + 1], in0=var_eps[:, t:t + 1], in1=minus_half, op=ALU.pow)
                if s != QMM:
                    power.then_inc(rstd_ready, 1)
                    return
                own(power)
                if nth[QMM][n]:
                    pool.wait_ge(y1_ready, nth[QMM][n])
                own(nc.gpsimd.tensor_tensor(out=q_scale, in0=rstd[:, t:t + 1], in1=inv_s1, op=ALU.mult))
                own(nc.gpsimd.tensor_tensor(out=q_mean, in0=mv[:, 2 * t:2 * t + 1], in1=q_scale, op=ALU.mult))
                nc.gpsimd.tensor_tensor(out=q_shift, in0=z1, in1=q_mean, op=ALU.subtract).then_inc(input_rstd_ready, 1)

            def add_vector(n):
                _, s, t = SEQ[n]
                xt = x_sb[:, t, :]
                if s == QMM:
                    pool.wait_ge(x_row_added, nth[QMM][n] + 1)
                    pool.wait_ge(col_term_ready, SEQ[n][0] + 1)
                else:
                    pool.wait_ge(rows_ready, nth_float[n] + 1)
                    pool.wait_ge(bias_in, 16 * (2 * SEQ[n][0] + (1 if s == FFN0 else 2)))
                nc.gpsimd.tensor_tensor(out=xt, in0=xt, in1=(col_term if s == QMM else bias)[:, :],
                                        op=ALU.add).then_inc(x_added, 1)

            def sum_q2(b, k):
                pool.wait_ge(unit_lo, unit_no["q2", b, k] + 1)
                if k == 1:
                    pool.wait_ge(x_added, nth_added[POS[b - 1, QMM, TILES - 1]] + 1)
                    pool.wait_ge(acc_done, POS[b - 1, FFN0, TILES - 1] + 1)
                    nc.gpsimd.tensor_copy(lowt_hi[:, :], ones16[:, :])
                before = q2[:, 0, :] if k == 1 else col_sum[:, :].bitcast(F32)
                last = nc.gpsimd.tensor_tensor(out=col_sum[:, :], in0=q2[:, k, :], in1=before, op=ALU.add)
                if k < KT - 1:
                    own(last)
                else:
                    last.then_inc(col_sum_ready, 1)

            def do_first_unit(k):
                pool.wait_ge(first_hi, KT + k + 1)
                nc.gpsimd.tensor_tensor(out=r0_lo[:, k, :], in0=first_w0[:, k, :], in1=r0_hi[:, k, :].bitcast(F32),
                                        op=ALU.subtract).then_inc(first_w0_lo_pool, 1)

            pool.wait_ge(scalars_ready, 1)
            inverse_deviation(POS[0, QMM, 0])
            inverse_deviation(POS[0, QMM, 1])
            do_first_unit(0)
            inverse_deviation(POS[0, QMM, 2])
            for n in range(N):
                if SEQ[n][1] == FFN0:
                    for k in first_w0_pool.get(n, []):
                        do_first_unit(k)
                if n in nth_added:
                    add_vector(n)
                if n and SEQ[n - 1][1] in NEXT_NORM:
                    b, s, t = SEQ[n - 1]
                    inverse_deviation(POS[b, NEXT_NORM[s], t])
                if SEQ[n][1] != FFN0:
                    for k in first_w0_pool.get(n, []):
                        do_first_unit(k)
                for b, k in SUM_Q2.get(n, []):
                    sum_q2(b, k)
                if n in NORM_X:
                    b, t = NORM_X[n]
                    inverse_deviation(POS[b, QMM, t])

        @block.vector
        def _(dve):
            steps = [0]

            def own(ins):
                steps[0] += 1
                ins.then_inc(dve_step, 1)
                dve.wait_ge(dve_step, steps[0])

            def norm_stats(n):
                _, s, t = SEQ[n]
                ready = input_var_ready if s == QMM else var_ready
                st = stats.rearrange("p (h c) -> p h c", h=2)
                nc.vector.bn_stats(out=st[:, 0, :], in_=x_sb[:, t, 0:HALF])
                own(nc.vector.bn_stats(out=st[:, 1, :], in_=x_sb[:, t, HALF:D]))
                own(nc.vector.bn_aggr(out=mv[:, 2 * t:2 * t + 2], in_=st))
                nc.vector.tensor_scalar(var_eps[:, t:t + 1], mv[:, 2 * t + 1:2 * t + 2], EPS, None,
                                        ALU.add).then_inc(ready, 1)
                dve.wait_ge(ready, norm_no(n) + 1)

            def round_q(dst, v):
                own(nc.vector.tensor_scalar(v, v, MAGIC, MAGIC, ALU.add, ALU.max))
                return nc.vector.tensor_scalar(dst, v, MAGIC + QMAX, MAGIC + MID, ALU.min, ALU.subtract)

            def make_rows(n):
                b, s, t = SEQ[n]
                if s == QMM:
                    if nth[QMM][n]:
                        before = [m for m in range(n) if SEQ[m][1] == QMM][-1]
                        dve.wait_ge(tr_done, 2 * before + 2)
                        dve.wait_ge(row_term_ready, nth[QMM][n])
                    dve.wait_ge(y1_ready, nth[QMM][n] + 1)
                    round_q(q1[:, :], rows[:, :]).then_inc(q1_ready, 1)
                    return
                if n:
                    if SEQ[n - 1][1] == QMM:
                        dve.wait_ge(q1_ready, nth[QMM][n - 1] + 1)
                    else:
                        dve.wait_ge(tr_done, 2 * (n - 1) + 2)
                if s == PV:
                    nc.vector.tensor_scalar(rows[:, :], e_sb[:, t, :], e_inv[:, t:t + 1], None,
                                            ALU.mult).then_inc(rows_ready, 1)
                    return
                dve.wait_ge(rstd_ready, norm_no(n) + 1)
                nc.vector.tensor_scalar(rows[:, :], x_sb[:, t, :], mv[:, 2 * t:2 * t + 1], rstd[:, t:t + 1],
                                        ALU.subtract, ALU.mult).then_inc(rows_ready, 1)

            def split_low_half(n):
                for h in range(2):
                    ks = slice(h * KH, (h + 1) * KH)
                    dve.wait_ge(hi_done, 2 * n + h + 1)
                    nc.vector.tensor_tensor(out=rt_lo[:, n % 2, ks, :],
                                            in0=tp[:, h, :].rearrange("p (k r) -> p k r", k=KH),
                                            in1=rt_hi[:, n % 2, ks, :].bitcast(F32),
                                            op=ALU.subtract).then_inc(lo_done, 1)

            def fold_unit(u):
                m, b, k = units[u]
                dve.wait_ge(raw_in[u % RAW], 16 * (u // RAW + 1))
                dve.wait_ge(fold_done, k + 1)
                for h, ps in enumerate((low_ps, lowt_ps)):
                    part = raw[:, u % RAW, h * HALF:(h + 1) * HALF]
                    both = nc.vector.tensor_tensor(out=part, in0=ps[:, :], in1=part, op=ALU.add)
                both.then_inc(folded, 1)

            def do_unit(u):
                m, b, k = units[u]
                src = unit_raw(u)
                dve.wait_ge(unit_hi, u + 1)
                if m == "q2":
                    dve.wait_ge(rows_ready, nth_float[POS[b - 1, PV, k // 2]] + 1)
                    round_q(q2[:, k, :], src).then_inc(unit_lo, 1)
                    return
                hi, lo = unit_dest(m, k)
                if m == "lora1a":
                    dve.wait_ge(coef_in, 16)
                    nc.vector.tensor_scalar(coef, coef_raw, SCALING, None, ALU.mult).then_inc(coef_ready, 1)
                if m == "lora1b":
                    dve.wait_ge(coef_ready, 1)
                    nc.vector.scalar_tensor_tensor(out=lo, in0=src, scalar=coef, in1=hi.bitcast(F32),
                                                   op0=ALU.mult, op1=ALU.subtract).then_inc(unit_lo, 1)
                else:
                    nc.vector.tensor_tensor(out=lo, in0=src, in1=hi.bitcast(F32), op=ALU.subtract).then_inc(unit_lo, 1)
                if m == "lora0a":
                    dve.wait_ge(gate_hi, b + 1)
                    nc.vector.tensor_tensor(out=a_parts[:, :, 1, ER:], in0=gate_raw[:, :, :],
                                            in1=a_parts[:, :, 0, ER:].bitcast(F32), op=ALU.subtract).then_inc(gate_lo, 1)

            def do_first_unit(k):
                dve.wait_ge(first_hi, KT + k + 1)
                nc.vector.tensor_tensor(out=r0_lo[:, k, :], in0=first_w0[:, k, :], in1=r0_hi[:, k, :].bitcast(F32),
                                        op=ALU.subtract).then_inc(first_w0_lo, 1)

            def column_term(b):
                if b:
                    dve.wait_ge(x_added, nth_added[POS[b - 1, QMM, TILES - 1]] + 1)
                dve.wait_ge(colsum_done, b + 1)
                nc.vector.tensor_scalar(col_term[:, 0:HALF], low_ps[:, :], col_add, col_f, ALU.add, ALU.mult)
                nc.vector.tensor_scalar(col_term[:, HALF:D], lowt_ps[:, :], col_add, col_f, ALU.add,
                                        ALU.mult).then_inc(col_term_ready, 1)

            def take_sums(n):
                b, s, t = SEQ[n]
                dve.wait_ge(acc_done, n + 1)
                a, xt = acc[:, n % 2, :], x_sb[:, t, :]
                if s == QK:
                    own(nc.vector.tensor_reduce(out=neg_max[:, 0:1], in_=a, axis=AX.X, op=ALU.max))
                    if nth[QK][n]:
                        dve.wait_ge(exp_done, nth[QK][n])
                    nc.vector.tensor_scalar(neg_max[:, 1:2], neg_max[:, 0:1], -1.0, None,
                                            ALU.mult).then_inc(max_ready, 1)
                    return
                if s != PV:
                    dve.wait_ge(x_added, nth_added[n] + 1)
                if s == QMM:
                    added = nc.vector.scalar_tensor_tensor(out=xt, in0=a, scalar=s12, in1=xt, op0=ALU.mult, op1=ALU.add)
                else:
                    added = nc.vector.tensor_tensor(out=xt, in0=a, in1=xt, op=ALU.add)
                added.then_inc(acc_free, 1)
                dve.wait_ge(acc_free, n + 1)

            def invert_sum(n):
                t = SEQ[n][2]
                dve.wait_ge(exp_done, nth[QK][n] + 1)
                nc.vector.reciprocal(e_inv[:, t:t + 1], e_sum[:, t:t + 1]).then_inc(acc_free, 1)
                dve.wait_ge(acc_free, n + 1)

            def low_rank(n):
                s = SEQ[n][1]
                dve.wait_ge(low_done, nth[FFN0][n] + 1)
                if nth[FFN0][n]:
                    dve.wait_ge(lowt_done, nth[FFN0][n])
                own(nc.vector.tensor_copy(low[:, :], low_ps[:, LOW:2 * LOW]))
                own(nc.vector.tensor_tensor(out=low[:, :], in0=low_ps[:, 0:LOW], in1=low[:, :], op=ALU.add))
                logits = low[:, ER:]
                own(nc.vector.max(out=top, in_=logits))
                nc.vector.max_index(out=idx[:, :], in_max=top, in_values=logits)
                nc.vector.tensor_tensor(out=gap, in0=top[:, 1:2], in1=top[:, 0:1], op=ALU.subtract).then_inc(gap_ready, 1)
                dve.wait_ge(gap_ready, nth[FFN0][n] + 1)
                own(nc.vector.tensor_copy(idx_f, idx[:, 0:TOP]))
                dve.wait_ge(gap_exp_ready, nth[FFN0][n] + 1)
                own(nc.vector.tensor_scalar(gap_den, gap_exp, 1.0, None, ALU.add))
                own(nc.vector.reciprocal(top_w[:, 0:1], gap_den))
                own(nc.vector.tensor_tensor(out=top_w[:, 1:2], in0=gap_exp, in1=top_w[:, 0:1], op=ALU.mult))
                for i in range(TOP):
                    oh = nc.vector.tensor_scalar(one_hot[:, i * EXPERTS:(i + 1) * EXPERTS], expert_no,
                                                 idx_f[:, i:i + 1], top_w[:, i:i + 1], ALU.is_equal, ALU.mult)
                own(oh)
                own(nc.vector.tensor_tensor(out=expert_w, in0=one_hot[:, 0:EXPERTS], in1=one_hot[:, EXPERTS:], op=ALU.add))
                nc.vector.scalar_tensor_tensor(
                    out=low_s[:, :].rearrange("p (e r) -> p e r", e=EXPERTS),
                    in0=low[:, 0:ER].rearrange("p (e r) -> p e r", e=EXPERTS), scalar=SCALING,
                    in1=expert_w.unsqueeze(2).to_broadcast([P, EXPERTS, RANK]),
                    op0=ALU.mult, op1=ALU.mult).then_inc(low_ready, 1)

            def split_low_rank(n):
                dve.wait_ge(lowt_hi_done, nth[FFN0][n] + 1)
                nc.vector.tensor_tensor(out=lowt_lo[:, :], in0=lowt_ps[:, 0:P], in1=lowt_hi[:, :].bitcast(F32),
                                        op=ALU.subtract).then_inc(lowt_lo_done, 1)

            dve.wait_ge(scalars_in, 16)
            nc.vector.reciprocal(inv_s1, s1)
            nc.vector.reciprocal(inv_s2, s2)
            nc.vector.tensor_scalar(d2, z2, -1.0, MID, ALU.mult, ALU.add)
            nc.vector.tensor_scalar(col_f, z1, -1.0, MID, ALU.mult, ALU.add)
            own(nc.vector.tensor_tensor(out=s12, in0=s1, in1=s2, op=ALU.mult))
            nc.vector.tensor_tensor(out=row_f, in0=s12, in1=d2, op=ALU.mult)
            nc.vector.tensor_tensor(out=col_f, in0=s12, in1=col_f, op=ALU.mult)
            nc.vector.tensor_scalar(col_add, d2, float(D), None, ALU.mult).then_inc(scalars_ready, 1)
            dve.wait_ge(scalars_ready, 1)
            dve.wait_ge(x_in[0], 16)
            norm_stats(POS[0, QMM, 0])
            for k in range(KT):
                if k == 1:
                    make_rows(0)
                if k == 3:
                    dve.wait_ge(x_in[1], 16)
                    norm_stats(POS[0, QMM, 1])
                if k == 5:
                    make_rows(1)
                dve.wait_ge(first_hi, k + 1)
                round_q(q2[:, k, :], first_ctx[:, k, :]).then_inc(first_q2, 1)
            dve.wait_ge(x_in[2], 16)
            norm_stats(POS[0, QMM, 2])
            dve.wait_ge(consts_ready, 1)
            for n in range(N):
                b, s, t = SEQ[n]
                nxt = n + 1
                todo = [("first", k) for k in first_w0_dve.get(n, [])]
                for u in window_units[n]:
                    todo += [("fold", unit_no[u])] * folds(u[0], u[1]) + [("split", unit_no[u])]

                def some(keep):
                    while len(todo) > keep:
                        what, u = todo.pop(0)
                        if what == "first":
                            do_first_unit(u)
                        elif what == "fold":
                            fold_unit(u)
                        else:
                            do_unit(u)

                if SEQ[n] == (0, FFN0, 0):
                    some(0)
                    low_rank(n)
                    make_rows(nxt)
                    split_low_rank(n)
                    make_rows(MAKE_LAST[n])
                rows_first = s == FFN1 and is_quant(nxt) and SEQ[n - 1][1] == QMM
                if rows_first:
                    make_rows(nxt)
                if n:
                    take_sums(n - 1)
                if s == QMM and not is_quant(nxt):
                    split_low_half(nxt)
                if n and SEQ[n - 1][1] in NEXT_NORM:
                    lb, ls, lt = SEQ[n - 1]
                    norm_stats(POS[lb, NEXT_NORM[ls], lt])
                if b and (s, t) == (QMM, 0):
                    column_term(b)
                if MAKE_FIRST[n] and not rows_first and SEQ[n] != (0, FFN0, 0):
                    if s == FFN1 and is_quant(nxt):
                        some(max(len(todo) - 1, 0))
                    make_rows(MAKE_FIRST[n])
                if s == FFN0 and SEQ[n] != (0, FFN0, 0):
                    some(max(len(todo) - 1, 0))
                    low_rank(n)
                if n and SEQ[n - 1][1] == QK:
                    invert_sum(n - 1)
                if s == PV:
                    some(max(len(todo) - 1, 0))
                elif s != QMM and not rows_first:
                    some(0 if len(todo) == 1 else len(todo) // 2)
                if nxt < N and s != QMM and not is_quant(nxt):
                    split_low_half(nxt)
                if s == FFN0 and SEQ[n] != (0, FFN0, 0):
                    split_low_rank(n)
                if n == 0:
                    column_term(0)
                if MAKE_LAST[n] and SEQ[n] != (0, FFN0, 0):
                    make_rows(MAKE_LAST[n])
                if s != QMM or not b:
                    some(0)
                if n in NORM_X:
                    nb, nt = NORM_X[n]
                    dve.wait_ge(x_in[nt], 16 * (nb + 1))
                    norm_stats(POS[nb, QMM, nt])
                some(0)
            dve.wait_ge(x_added, nth_added[N - 1] + 1)
            for h in range(2):
                dve.wait_ge(acc_done, N + h)
                xt = x_sb[:, SEQ[N - 1][2], h * HALF:(h + 1) * HALF]
                nc.vector.tensor_tensor(out=xt, in0=acc[:, (N - 1) % 2, h * HALF:(h + 1) * HALF], in1=xt,
                                        op=ALU.add).then_inc(acc_free, 1)

        @block.scalar
        def _(act):
            def scale_rows(n):
                t = SEQ[n][2]
                act.wait_ge(input_rstd_ready, nth[QMM][n] + 1)
                if n:
                    if SEQ[n - 1][1] == QMM:
                        act.wait_ge(q1_ready, nth[QMM][n - 1] + 1)
                    else:
                        act.wait_ge(tr_done, 2 * (n - 1) + 2)
                nc.scalar.activation(rows[:, :], x_sb[:, t, :], ACT.Identity, bias=q_shift,
                                     scale=q_scale).then_inc(y1_ready, 1)

            def add_row_term(n):
                t = SEQ[n][2]
                act.wait_ge(tr_done, 2 * n + 2)
                nc.scalar.activation(q1[:, :], q1[:, :], ACT.Copy, scale=row_f,
                                     accum_out=row_term[:, t:t + 1]).then_inc(row_term_ready, 1)
                act.wait_ge(row_term_ready, nth[QMM][n] + 1)
                nc.scalar.activation(x_sb[:, t, :], x_sb[:, t, :], ACT.Identity,
                                     bias=row_term[:, t:t + 1]).then_inc(x_row_added, 1)

            def split_high_half(n):
                s = SEQ[n][1]
                for h in range(2):
                    ks = slice(h * KH, (h + 1) * KH)
                    act.wait_ge(tr_done, 2 * n + h + 1)
                    if s == QMM:
                        src = tp[:, h, 0:HALF // 2].bitcast(BF16).rearrange("p (k r) -> p k r", k=KH)
                        dst = q1_t[n % 2][:, ks, :]
                    else:
                        src = tp[:, h, :].rearrange("p (k r) -> p k r", k=KH)
                        dst = rt_hi[:, n % 2, ks, :]
                    nc.scalar.activation(dst, src, ACT.Copy).then_inc(hi_done, 1)

            def do_unit(u):
                m, b, k = units[u]
                src = unit_raw(u)
                act.wait_ge(raw_in[u % RAW], 16 * (u // RAW + 1))
                if folds(m, b):
                    act.wait_ge(folded, k + 1)
                    act.dma_start(w1_folded[k * P:(k + 1) * P, :], src).then_inc(folded_stored[u % RAW], 16)
                reader = last_reader(m, b)
                if reader is not None:
                    act.wait_ge(acc_done, reader + 1)
                if m == "kt" and b == 0:
                    act.wait_ge(first_w0_lo, len(DVE_W0))
                    act.wait_ge(first_w0_lo_pool, len(POOL_W0))
                if m == "q2":
                    nc.scalar.activation(src, src, ACT.Identity, bias=z2, scale=inv_s2).then_inc(unit_hi, 1)
                    return
                hi, _ = unit_dest(m, k)
                if m == "lora1b":
                    act.wait_ge(coef_ready, 1)
                scale = coef if m == "lora1b" else 1.0
                nc.scalar.activation(hi, src, ACT.Copy, scale=scale).then_inc(unit_hi, 1)
                if m == "lora0a":
                    act.wait_ge(gate_in, 16)
                    nc.scalar.activation(a_parts[:, :, 0, ER:], gate_raw[:, :, :], ACT.Copy).then_inc(gate_hi, 1)

            def do_first_unit(k):
                act.wait_ge(first_w0_in[k], 16)
                nc.scalar.activation(r0_hi[:, k, :], first_w0[:, k, :], ACT.Copy).then_inc(first_hi, 1)

            def exponentials(n):
                t = SEQ[n][2]
                act.wait_ge(max_ready, nth[QK][n] + 1)
                nc.scalar.activation(e_sb[:, t, :], acc[:, n % 2, :], ACT.Exp, bias=neg_max[:, 1:2],
                                     accum_out=e_sum[:, t:t + 1]).then_inc(exp_done, 1)

            def gap_exponential(n):
                act.wait_ge(gap_ready, nth[FFN0][n] + 1)
                nc.scalar.activation(gap_exp, gap, ACT.Exp).then_inc(gap_exp_ready, 1)

            def load_bias(b, s):
                if (b, s) != (0, FFN0):
                    last = (b - 1, FFN1, TILES - 1) if s == FFN0 else (b, FFN0, TILES - 1)
                    act.wait_ge(x_added, nth_added[POS[last]] + 1)
                act.dma_start(bias[:, :], (b0 if s == FFN0 else b1).partition_broadcast(P)).then_inc(bias_in, 16)

            def load_x(n):
                lb, lt = LOAD_X[n]
                act.wait_ge(out_done[lt], 16 * lb)
                act.dma_start(x_sb[:, lt, :], x[lb, lt * P:(lt + 1) * P, :]).then_inc(x_in[lt], 16)

            def store(n):
                b, _, t = SEQ[n]
                act.wait_ge(acc_free, n + 1)
                act.dma_start(out[b, t * P:(t + 1) * P, :], x_sb[:, t, :]).then_inc(out_done[t], 16)

            act.wait_ge(consts_ready, 1)
            nc.scalar.activation(gap_exp, minus_half, ACT.Exp).then_inc(table_loaded, 1)
            act.wait_ge(scalars_ready, 1)
            for k in range(KT):
                if k == 1:
                    scale_rows(0)
                if k == 3:
                    split_high_half(0)
                if k == 4:
                    add_row_term(0)
                if k == 5:
                    scale_rows(1)
                act.wait_ge(first_ctx_in[k], 16)
                nc.scalar.activation(first_ctx[:, k, :], first_ctx[:, k, :], ACT.Identity, bias=z2,
                                     scale=inv_s2).then_inc(first_hi, 1)
            do_first_unit(0)
            for n in range(N):
                b, s, t = SEQ[n]
                nxt = n + 1
                todo = [("split", unit_no[u]) for u in window_units[n]] + [("first", k) for k in first_w0_hi.get(n, [])]

                def some(keep):
                    while len(todo) > keep:
                        what, u = todo.pop(0)
                        if what == "first":
                            do_first_unit(u)
                        else:
                            do_unit(u)

                if n and SEQ[n - 1][1] == QK:
                    exponentials(n - 1)
                if MAKE_FIRST[n] and is_quant(nxt):
                    if s == FFN1 and SEQ[n - 1][1] == FFN1:
                        some(0)
                    if SEQ[n] == (0, FFN0, 0):
                        gap_exponential(n)
                    scale_rows(nxt)
                if n in LOAD_X and SEQ[n - 1][1] != FFN1:
                    load_x(n)
                if s == FFN0:
                    some(max(len(todo) - 1, 0))
                    if SEQ[n] != (0, FFN0, 0):
                        gap_exponential(n)
                if s == PV:
                    some(max(len(todo) - 1, 0) if folds("w1", b) else len(todo) // 2)
                elif s != QMM:
                    some(0 if len(todo) == 1 else len(todo) // 2)
                if s == FFN1 and SEQ[n - 1][1] == FFN1:
                    store(n - 1)
                if nxt < N and not (s == FFN0 and TRANSPOSE_AT[n] == KT):
                    split_high_half(nxt)
                if s == FFN0:
                    act.wait_ge(lowt_done, nth[FFN0][n] + 1)
                    nc.scalar.activation(lowt_hi[:, :], lowt_ps[:, 0:P], ACT.Copy).then_inc(lowt_hi_done, 1)
                if s == FFN0 and TRANSPOSE_AT[n] == KT:
                    split_high_half(nxt)
                if is_quant(nxt):
                    add_row_term(nxt)
                if n in LOAD_BIAS:
                    load_bias(*LOAD_BIAS[n])
                if s != FFN1 and n and SEQ[n - 1][1] == FFN1:
                    store(n - 1)
                if n in LOAD_X and SEQ[n - 1][1] == FFN1:
                    load_x(n)
                if MAKE_LAST[n] and is_quant(MAKE_LAST[n]):
                    scale_rows(MAKE_LAST[n])
                some(0)
            b, _, t = SEQ[N - 1]
            for h in range(2):
                act.wait_ge(acc_free, N + h)
                cs = slice(h * HALF, (h + 1) * HALF)
                act.dma_start(out[b, t * P:(t + 1) * P, cs], x_sb[:, t, cs]).then_inc(out_done[t], 16)
            for i in range(TILES):
                act.wait_ge(out_done[i], 16 * (BATCHES + (i == t)))

        @block.tensor
        def _(pe):
            def transposes(n):
                s = SEQ[n][1]
                if s == QMM:
                    pe.wait_ge(q1_ready, nth[QMM][n] + 1)
                else:
                    pe.wait_ge(rows_ready, nth_float[n] + 1)
                for h in range(2):
                    for i in range(KH):
                        k = h * KH + i
                        if s == QMM:
                            dst = tp[:, h, 0:HALF // 2].bitcast(BF16)[:, i * P:(i + 1) * P]
                            last = nc.tensor.transpose(dst, q1[:, k * P:(k + 1) * P], ident16[:, :])
                        else:
                            last = nc.tensor.transpose(tp[:, h, i * P:(i + 1) * P],
                                                       rows[:, k * P:(k + 1) * P], ident[:, :])
                    last.then_inc(tr_done, 1)

            def matrix_ready(s, b, k):
                if s == FFN0 and b == 0:
                    if k in POOL_W0:
                        pe.wait_ge(first_w0_lo_pool, POOL_W0.index(k) + 1)
                    else:
                        pe.wait_ge(first_w0_lo, DVE_W0.index(k) + 1)
                elif s == QMM and b == 0:
                    pe.wait_ge(first_q2, k + 1)
                else:
                    m = {QMM: "q2", FFN0: "w0", QK: "kt", PV: "v", FFN1: "w1"}[s]
                    pe.wait_ge(unit_lo, unit_no[m, b, k] + 1)

            def rows_split(n, h):
                if SEQ[n][1] == QMM:
                    pe.wait_ge(hi_done, 2 * n + h + 1)
                else:
                    pe.wait_ge(lo_done, 2 * nth_float[n] + h + 1)

            def column_sums(b, k):
                for h, dst in enumerate((low_ps, lowt_ps)):
                    last = nc.tensor.matmul(dst[:, :], ones16[:, :], q2[:, k, h * HALF:(h + 1) * HALF],
                                            start=(k == 0), stop=(k == KT - 1))
                if k == KT - 1:
                    last.then_inc(colsum_done, 1)

            PASSES = ((0, 0), (0, 1), (1, 0))

            def fold(k):
                if k == 0:
                    pe.wait_ge(unit_lo, unit_no["lora1b", 0, 0] + 1)
                else:
                    pe.wait_ge(folded, k)
                for h, dst in enumerate((low_ps, lowt_ps)):
                    for i, (l, r) in enumerate(PASSES):
                        last = nc.tensor.matmul(dst[:, :], a_parts[:, k, l, 0:P], (bb_hi, bb_lo)[r][:, h * HALF:(h + 1) * HALF],
                                                start=(i == 0), stop=(i == 2))
                last.then_inc(fold_done, 1)

            pe.wait_ge(consts_ready, 1)
            transposes(0)
            for n in range(N):
                b, s, t = SEQ[n]
                p = n % 2
                left = (rt_hi, rt_lo)
                right = {FFN0: (r0_hi, r0_lo), QK: (r1_hi, r1_lo), PV: (r0_hi, r0_lo), FFN1: (r1_hi, r1_lo)}.get(s)
                to_fold = [k for m, ub, k in window_units[n] if folds(m, ub)]
                rows_split(n, 0)
                if n >= 2:
                    pe.wait_ge(acc_free, n - 1)
                for k in range(KT):
                    if k == TRANSPOSE_AT[n] and n + 1 < N:
                        rows_split(n, 1)
                        transposes(n + 1)
                    if k == KH:
                        rows_split(n, 1)
                    if t == 0:
                        matrix_ready(s, b, k)
                    if b and (s, t, k) == (QMM, 0, KH):
                        pe.wait_ge(col_sum_ready, b)
                        for h, dst in enumerate((low_ps, lowt_ps)):
                            last = nc.tensor.matmul(dst[:, :], lowt_hi[:, :], col_sum[:, h * HALF:(h + 1) * HALF],
                                                    start=True, stop=True)
                        last.then_inc(colsum_done, 1)
                    if s == QMM:
                        if n == 0:
                            column_sums(b, k)
                        for h in range(2):
                            last = nc.tensor.matmul(acc[:, p, h * HALF:(h + 1) * HALF], q1_t[p][:, k, :],
                                                    q2[:, k, h * HALF:(h + 1) * HALF], start=(k == 0), stop=(k == KT - 1))
                        continue
                    if n == N - 1:
                        continue
                    if to_fold and k % KH == 1:
                        fold(to_fold.pop(0))
                    end = k == KT - 1 and s != FFN0
                    for i, (l, r) in enumerate(PASSES):
                        for h in range(2):
                            last = nc.tensor.matmul(acc[:, p, h * HALF:(h + 1) * HALF], left[l][:, p, k, :],
                                                    right[r][:, k, h * HALF:(h + 1) * HALF],
                                                    start=(k == 0 and i == 0), stop=(end and i == 2))
                    if s == FFN0 and k == LOW_AT[n]:
                        rows_split(n, 1)
                        if t == 0:
                            pe.wait_ge(unit_lo, unit_no["lora0a", b, 0] + 1)
                            pe.wait_ge(gate_lo, b + 1)
                            pe.wait_ge(col_term_ready, b + 1)
                        for kk in range(KT):
                            nc.tensor.matmul(low_ps[:, 0:2 * LOW], rt_hi[:, p, kk, :],
                                             a_parts[:, kk, :, :].rearrange("p c e -> p (c e)"),
                                             start=(kk == 0), stop=False)
                            low_last = nc.tensor.matmul(low_ps[:, 0:LOW], rt_lo[:, p, kk, :], a_parts[:, kk, 0, :],
                                                        start=False, stop=(kk == KT - 1))
                        low_last.then_inc(low_done, 1)
                    if s == FFN0 and k == LOWT_AT[n]:
                        pe.wait_ge(low_ready, nth[FFN0][n] + 1)
                        nc.tensor.transpose(lowt_ps[:, 0:P], low_s[:, :], ident[:, :]).then_inc(lowt_done, 1)
                if s == FFN0 and TRANSPOSE_AT[n] == KT:
                    transposes(n + 1)
                if s == FFN0:
                    if t == 0:
                        pe.wait_ge(unit_lo, unit_no["lora0b", b, 0] + 1)
                    pe.wait_ge(lowt_lo_done, nth[FFN0][n] + 1)
                    lt = (lowt_hi, lowt_lo)
                    for i, (l, r) in enumerate(PASSES):
                        for h in range(2):
                            last = nc.tensor.matmul(acc[:, p, h * HALF:(h + 1) * HALF], lt[l][:, :],
                                                    (bb_hi, bb_lo)[r][:, h * HALF:(h + 1) * HALF], start=False, stop=(i == 2))
                if n == N - 1:
                    for h in range(2):
                        for k in range(KT):
                            for i, (l, r) in enumerate(PASSES):
                                last = nc.tensor.matmul(acc[:, p, h * HALF:(h + 1) * HALF], left[l][:, p, k, :],
                                                        right[r][:, k, h * HALF:(h + 1) * HALF],
                                                        start=(k == 0 and i == 0), stop=(k == KT - 1 and i == 2))
                        last.then_inc(acc_done, 1)
                    continue
                last.then_inc(acc_done, 1)
                if s != FFN0 and TRANSPOSE_AT[n] == KT:
                    transposes(n + 1)


def kernel(x, ctx_4096, L0_xattn_x1_scale, L0_xattn_x1_zp, L0_xattn_x2_scale, L0_xattn_x2_zp, L0_ffn_gate_w,
           L0_ffn_base_w, L0_ffn_base_b, L0_ffn_lora_A, L0_ffn_lora_B, L1_ffn_lora_A, L1_ffn_lora_B, L1_ffn_W,
           L1_ffn_bias, L1_ffn_lora_weights):
    import numpy as np
    import concourse.bacc as bacc
    from concourse.bass_utils import run_bass_kernel_spmd

    P = 128
    c = np.ascontiguousarray

    def k_tiles(m):
        m = np.asarray(m)
        return c(m.reshape(-1, P, m.shape[1]).transpose(1, 0, 2).reshape(P, -1))

    lora_a_t = lambda a: k_tiles(np.asarray(a).reshape(-1, a.shape[2]).T)
    lora_b_t = lambda a: c(np.asarray(a).transpose(0, 2, 1).reshape(-1, a.shape[1]))
    rank = L1_ffn_lora_A.shape[1]
    arrays = {
        "x": c(x), "ctx": c(ctx_4096), "ctx_t": c(np.asarray(ctx_4096).transpose(0, 2, 1)),
        "q_scalars": np.concatenate([L0_xattn_x1_scale, L0_xattn_x1_zp, L0_xattn_x2_scale, L0_xattn_x2_zp]),
        "gate_t": k_tiles(np.asarray(L0_ffn_gate_w).T), "w0_t": c(np.asarray(L0_ffn_base_w).T), "b0": c(L0_ffn_base_b),
        "a0_t": lora_a_t(L0_ffn_lora_A), "bb0_t": lora_b_t(L0_ffn_lora_B),
        "a1": c(np.asarray(L1_ffn_lora_A).reshape(-1, L1_ffn_lora_A.shape[2])), "bb1_t": lora_b_t(L1_ffn_lora_B),
        "w1_t": c(np.asarray(L1_ffn_W).T), "b1": c(L1_ffn_bias),
        "lora_w": c(np.repeat(np.asarray(L1_ffn_lora_weights), rank).reshape(-1, 1)),
    }
    nc = bacc.Bacc("TRN2", target_bir_lowering=False, num_devices=1, dynamic_dma_scratch_size=1024)
    dram = {n: nc.dram_tensor(n, a.shape, mybir.dt.from_np(a.dtype), kind="ExternalInput").ap() for n, a in arrays.items()}
    out = nc.dram_tensor("out", arrays["x"].shape, mybir.dt.float32, kind="ExternalOutput").ap()
    g = dram["gate_t"].rearrange("p (k e) -> p k e", e=L0_ffn_gate_w.shape[0])
    two_layer_kernel(nc, dram["x"], dram["ctx"], dram["ctx_t"], dram["q_scalars"], g,
                     dram["w0_t"], dram["b0"], dram["a0_t"], dram["bb0_t"], dram["a1"], dram["bb1_t"], dram["w1_t"],
                     dram["b1"], dram["lora_w"], out)
    got = run_bass_kernel_spmd(nc, [arrays], core_ids=[0])
    return got.results[0]["out"]
```
